# Optimizing a Trainium2 kernel written in Bass

```python
import numpy as np
import jax
import jax.numpy as jnp

def _softmax(x, axis=-1):
    return jax.nn.softmax(x, axis=axis)

def _gelu(x):
    return jax.nn.gelu(x, approximate=True)

def _silu(x):
    return jax.nn.silu(x)

def _sigmoid(x):
    return jax.nn.sigmoid(x)

def _layernorm(x, axis=-1, eps=1e-05):
    m = jnp.mean(x, axis=axis, keepdims=True)
    v = jnp.var(x, axis=axis, keepdims=True)
    return (x - m) / jnp.sqrt(v + eps)

def _scatter_add(tgt, idx, src, axis=0):
    return tgt.at[idx].add(src)

def _segment_sum(src, seg, n):
    return jax.ops.segment_sum(src, seg, n)
kernel_name = 'mk_gnn_resnorm_d4_gnn_r8_54fa87'

def setup_inputs(seed: int=0):
    np.random.seed(seed)
    _w = jnp.asarray

    def _rec_inputs():
        import jax
        import jax.numpy as jnp
        _gk = jax.random.key(seed)
        x = -0.0001006 + 1 * jax.random.normal(jax.random.fold_in(_gk, 1), (12500, 96), jnp.float32)
        src = jax.random.randint(jax.random.fold_in(_gk, 2), (200000,), 0, 12500, jnp.int32)
        dst = jax.random.randint(jax.random.fold_in(_gk, 3), (200000,), 0, 12500, jnp.int32)
        _o = jnp.argsort(dst, stable=True)
        src = src[_o]
        dst = dst[_o]
        edge_attr_32 = 0.000196303 + 1.00016 * jax.random.normal(jax.random.fold_in(_gk, 12), (200000, 32), jnp.float32)
        edge_weight = jax.random.uniform(jax.random.fold_in(_gk, 14), (200000,), jnp.float32, 0.0, 0.999998)
        return (x, src, dst, edge_attr_32, edge_weight)
    x, src, dst, edge_attr_32, edge_weight = _rec_inputs()

    def _L0_gnn_setup():
        import jax, jax.numpy as jnp
        import numpy as np
        N, E = (6250, 100000)
        ND, ED = (96, 32)

        def _gelu(x):
            return jax.nn.gelu(x, approximate=False)
        key = jax.random.key(seed)
        ks = jax.random.split(key, 16)
        s = lambda fan_in: 1.0 / np.sqrt(fan_in)
        inp = {'x': jax.random.normal(ks[0], (N, ND), jnp.float32), 'edge_index': jax.random.randint(ks[1], (2, E), 0, N, jnp.int32), 'edge_attr': jax.random.normal(ks[2], (E, ED), jnp.float32), 'mW1': jax.random.uniform(ks[3], (ND + ED, ND), jnp.float32, -s(ND + ED), s(ND + ED)), 'mb1': jnp.zeros((ND,), jnp.float32), 'mW2': jax.random.uniform(ks[4], (ND, ND), jnp.float32, -s(ND), s(ND)), 'mb2': jnp.zeros((ND,), jnp.float32), 'gW1': jax.random.uniform(ks[5], (ND + ED, ND), jnp.float32, -s(ND + ED), s(ND + ED)), 'gb1': jnp.zeros((ND,), jnp.float32), 'gW2': jax.random.uniform(ks[6], (ND, 1), jnp.float32, -s(ND), s(ND)), 'gb2': jnp.zeros((1,), jnp.float32), 'uW1': jax.random.uniform(ks[7], (2 * ND, ND), jnp.float32, -s(2 * ND), s(2 * ND)), 'ub1': jnp.zeros((ND,), jnp.float32), 'uW2': jax.random.uniform(ks[8], (ND, ND), jnp.float32, -s(ND), s(ND)), 'ub2': jnp.zeros((ND,), jnp.float32), 'ln_g': jnp.ones((ND,), jnp.float32), 'ln_b': jnp.zeros((ND,), jnp.float32)}
        return inp
    _L0_gnn_all = _L0_gnn_setup()
    _L0_gnn_in = {k: v for k, v in _L0_gnn_all.items() if k in ('mW1', 'mb1', 'mW2', 'mb2', 'gW1', 'gb1', 'gW2', 'gb2', 'uW1', 'ub1', 'uW2', 'ub2', 'ln_g', 'ln_b')}
    del _L0_gnn_all

    def _L1_gnn_setup():
        import jax, jax.numpy as jnp
        import numpy as np
        N_NODES = 6250
        N_EDGES = 100000
        D_FEAT = 96
        key = jax.random.key(seed)
        k1, k2, k3 = jax.random.split(key, 3)
        X = jax.random.normal(k1, (N_NODES, D_FEAT), dtype=jnp.float32)
        edge_index = jax.random.randint(k2, (2, N_EDGES), 0, N_NODES, dtype=jnp.int64)
        edge_weight = jax.random.uniform(k3, (N_EDGES,), dtype=jnp.float32)
        return {'X': X, 'edge_index': edge_index, 'edge_weight': edge_weight}
    _L1_gnn_all = _L1_gnn_setup()
    _L1_gnn_in = {k: v for k, v in _L1_gnn_all.items() if k in ()}
    del _L1_gnn_all

    def _L2_gnn_setup():
        import jax, jax.numpy as jnp
        import numpy as np
        N_NODES = 12500
        N_EDGES = 100000
        D = 96
        BN_EPS = 1e-05
        LEAKY_SLOPE = 0.05

        def _gcn_norm(edge_index, n_nodes, dtype):
            loop = jnp.arange(n_nodes, dtype=edge_index.dtype)
            src = jnp.concatenate([edge_index[0], loop])
            dst = jnp.concatenate([edge_index[1], loop])
            deg = jax.ops.segment_sum(jnp.ones(src.shape, dtype=dtype), dst, num_segments=n_nodes)
            dinv = jnp.where(deg > 0, jax.lax.rsqrt(jnp.maximum(deg, 1e-12)), 0.0)
            norm = dinv[src] * dinv[dst]
            return (src, dst, norm)

        def _gcn_conv(x, W, b, src, dst, norm, n_nodes):
            h = x @ W
            msg = h[src] * norm[:, None]
            agg = jax.ops.segment_sum(msg, dst, num_segments=n_nodes)
            return agg + b
        key = jax.random.key(seed)
        ks = jax.random.split(key, 6)
        node_feat = jax.random.normal(ks[0], (N_NODES, D), dtype=jnp.float32)
        edge_index = jax.random.randint(ks[1], (2, N_EDGES), 0, N_NODES, dtype=jnp.int64)
        W1 = jax.random.normal(ks[2], (D, D), dtype=jnp.float32) / np.sqrt(D)
        b1 = jnp.zeros((D,), dtype=jnp.float32)
        W2 = jax.random.normal(ks[3], (D, D), dtype=jnp.float32) / np.sqrt(D)
        b2 = jnp.zeros((D,), dtype=jnp.float32)
        bn_gamma = jnp.ones((D,), dtype=jnp.float32)
        bn_beta = jnp.zeros((D,), dtype=jnp.float32)
        bn_mean = jnp.zeros((D,), dtype=jnp.float32)
        bn_var = jax.random.uniform(ks[4], (D,), dtype=jnp.float32, minval=0.5, maxval=1.5)
        return {'node_feat': node_feat, 'edge_index': edge_index, 'W1': W1, 'b1': b1, 'W2': W2, 'b2': b2, 'bn_gamma': bn_gamma, 'bn_beta': bn_beta, 'bn_mean': bn_mean, 'bn_var': bn_var}
    _L2_gnn_all = _L2_gnn_setup()
    _L2_gnn_in = {k: v for k, v in _L2_gnn_all.items() if k in ('W1', 'b1', 'W2', 'b2', 'bn_gamma', 'bn_beta', 'bn_mean', 'bn_var')}
    del _L2_gnn_all

    def _L3_gnn_setup():
        import jax, jax.numpy as jnp
        import numpy as np
        N_NODES = 6250
        N_EDGES = 100000
        D_FEAT = 96
        D_OUT = 96
        key = jax.random.key(seed)
        ks = jax.random.split(key, 6)
        feat = jax.random.normal(ks[0], (N_NODES, D_FEAT), dtype=jnp.float32)
        affine = jax.random.uniform(ks[1], (N_EDGES,), dtype=jnp.float32)
        mlp_w = jax.random.normal(ks[2], (D_OUT, 2 * D_FEAT), dtype=jnp.float32) * (1.0 / np.sqrt(2 * D_FEAT))
        mlp_b = jax.random.normal(ks[3], (D_OUT,), dtype=jnp.float32) * 0.01
        src_idx = jax.random.randint(ks[4], (N_EDGES,), 0, N_NODES, dtype=jnp.int64)
        dst_idx = jax.random.randint(ks[5], (N_EDGES,), 0, N_NODES, dtype=jnp.int64)
        return {'feat': feat, 'affine': affine, 'mlp_w': mlp_w, 'mlp_b': mlp_b, 'src_idx': src_idx, 'dst_idx': dst_idx}
    _L3_gnn_all = _L3_gnn_setup()
    _L3_gnn_in = {k: v for k, v in _L3_gnn_all.items() if k in ('mlp_w', 'mlp_b')}
    del _L3_gnn_all
    return {'x': x, 'src': src, 'dst': dst, 'edge_attr_32': edge_attr_32, 'edge_weight': edge_weight, 'L0_gnn_mW1': _L0_gnn_in['mW1'], 'L0_gnn_mb1': _L0_gnn_in['mb1'], 'L0_gnn_mW2': _L0_gnn_in['mW2'], 'L0_gnn_mb2': _L0_gnn_in['mb2'], 'L0_gnn_gW1': _L0_gnn_in['gW1'], 'L0_gnn_gb1': _L0_gnn_in['gb1'], 'L0_gnn_gW2': _L0_gnn_in['gW2'], 'L0_gnn_gb2': _L0_gnn_in['gb2'], 'L0_gnn_uW1': _L0_gnn_in['uW1'], 'L0_gnn_ub1': _L0_gnn_in['ub1'], 'L0_gnn_uW2': _L0_gnn_in['uW2'], 'L0_gnn_ub2': _L0_gnn_in['ub2'], 'L0_gnn_ln_g': _L0_gnn_in['ln_g'], 'L0_gnn_ln_b': _L0_gnn_in['ln_b'], 'L2_gnn_W1': _L2_gnn_in['W1'], 'L2_gnn_b1': _L2_gnn_in['b1'], 'L2_gnn_W2': _L2_gnn_in['W2'], 'L2_gnn_b2': _L2_gnn_in['b2'], 'L2_gnn_bn_gamma': _L2_gnn_in['bn_gamma'], 'L2_gnn_bn_beta': _L2_gnn_in['bn_beta'], 'L2_gnn_bn_mean': _L2_gnn_in['bn_mean'], 'L2_gnn_bn_var': _L2_gnn_in['bn_var'], 'L3_gnn_mlp_w': _L3_gnn_in['mlp_w'], 'L3_gnn_mlp_b': _L3_gnn_in['mlp_b']}

def reference(x, src, dst, edge_attr_32, edge_weight, L0_gnn_mW1, L0_gnn_mb1, L0_gnn_mW2, L0_gnn_mb2, L0_gnn_gW1, L0_gnn_gb1, L0_gnn_gW2, L0_gnn_gb2, L0_gnn_uW1, L0_gnn_ub1, L0_gnn_uW2, L0_gnn_ub2, L0_gnn_ln_g, L0_gnn_ln_b, L2_gnn_W1, L2_gnn_b1, L2_gnn_W2, L2_gnn_b2, L2_gnn_bn_gamma, L2_gnn_bn_beta, L2_gnn_bn_mean, L2_gnn_bn_var, L3_gnn_mlp_w, L3_gnn_mlp_b):
    import jax
    import jax.numpy as jnp

    def _L0_gnn_ref(x, edge_index, edge_attr, mW1, mb1, mW2, mb2, gW1, gb1, gW2, gb2, uW1, ub1, uW2, ub2, ln_g, ln_b):
        import jax, jax.numpy as jnp
        import numpy as np
        N, E = (6250, 100000)
        ND, ED = (96, 32)

        def _gelu(x):
            return jax.nn.gelu(x, approximate=False)
        src, dst = (edge_index[0], edge_index[1])
        edge_input = jnp.concatenate([x[src], edge_attr], axis=-1)
        messages = _gelu(edge_input @ mW1 + mb1) @ mW2 + mb2
        gates = jax.nn.sigmoid(_gelu(edge_input @ gW1 + gb1) @ gW2 + gb2)
        aggregated = jax.ops.segment_sum(messages * gates, dst, num_segments=x.shape[0])
        combined = jnp.concatenate([x, aggregated], axis=-1)
        update = _gelu(combined @ uW1 + ub1) @ uW2 + ub2
        h = x + update
        mu = jnp.mean(h, axis=-1, keepdims=True)
        var = jnp.mean(jnp.square(h - mu), axis=-1, keepdims=True)
        return (h - mu) * jax.lax.rsqrt(var + 1e-05) * ln_g + ln_b

    def _L1_gnn_ref(X, edge_index, edge_weight):
        import jax, jax.numpy as jnp
        import numpy as np
        N_NODES = 6250
        N_EDGES = 100000
        D_FEAT = 96
        dst, src = (edge_index[0], edge_index[1])
        messages = edge_weight[:, None] * X[src]
        out = jax.ops.segment_sum(messages, dst, num_segments=X.shape[0])
        return out

    def _L2_gnn_ref(node_feat, edge_index, W1, b1, W2, b2, bn_gamma, bn_beta, bn_mean, bn_var):
        import jax, jax.numpy as jnp
        import numpy as np
        N_NODES = 12500
        N_EDGES = 100000
        D = 96
        BN_EPS = 1e-05
        LEAKY_SLOPE = 0.05

        def _gcn_norm(edge_index, n_nodes, dtype):
            loop = jnp.arange(n_nodes, dtype=edge_index.dtype)
            src = jnp.concatenate([edge_index[0], loop])
            dst = jnp.concatenate([edge_index[1], loop])
            deg = jax.ops.segment_sum(jnp.ones(src.shape, dtype=dtype), dst, num_segments=n_nodes)
            dinv = jnp.where(deg > 0, jax.lax.rsqrt(jnp.maximum(deg, 1e-12)), 0.0)
            norm = dinv[src] * dinv[dst]
            return (src, dst, norm)

        def _gcn_conv(x, W, b, src, dst, norm, n_nodes):
            h = x @ W
            msg = h[src] * norm[:, None]
            agg = jax.ops.segment_sum(msg, dst, num_segments=n_nodes)
            return agg + b
        n = node_feat.shape[0]
        src, dst, norm = _gcn_norm(edge_index, n, node_feat.dtype)
        x = _gcn_conv(node_feat, W1, b1, src, dst, norm, n)
        x = jnp.where(x >= 0, x, LEAKY_SLOPE * x)
        x = (x - bn_mean) * jax.lax.rsqrt(bn_var + BN_EPS) * bn_gamma + bn_beta
        x = _gcn_conv(x, W2, b2, src, dst, norm, n)
        return x

    def _L3_gnn_ref(feat, affine, mlp_w, mlp_b, src_idx, dst_idx):
        import jax, jax.numpy as jnp
        import numpy as np
        N_NODES = 6250
        N_EDGES = 100000
        D_FEAT = 96
        D_OUT = 96
        msgs = feat[src_idx] * affine[:, None]
        agg = jax.ops.segment_sum(msgs, dst_idx, num_segments=feat.shape[0])
        gcn_feat = jnp.concatenate([feat, agg], axis=-1)
        out = gcn_feat @ mlp_w.T + mlp_b
        return out
    edge_index = jnp.stack([src, dst])
    x = _layernorm(x + _L0_gnn_ref(x, edge_index, edge_attr_32, L0_gnn_mW1, L0_gnn_mb1, L0_gnn_mW2, L0_gnn_mb2, L0_gnn_gW1, L0_gnn_gb1, L0_gnn_gW2, L0_gnn_gb2, L0_gnn_uW1, L0_gnn_ub1, L0_gnn_uW2, L0_gnn_ub2, L0_gnn_ln_g, L0_gnn_ln_b), axis=-1)
    x = _layernorm(x + _L1_gnn_ref(x, edge_index, edge_weight), axis=-1)
    x = _layernorm(x + _L2_gnn_ref(x, edge_index, L2_gnn_W1, L2_gnn_b1, L2_gnn_W2, L2_gnn_b2, L2_gnn_bn_gamma, L2_gnn_bn_beta, L2_gnn_bn_mean, L2_gnn_bn_var), axis=-1)
    x = _layernorm(x + _L3_gnn_ref(x, edge_weight, L3_gnn_mlp_w, L3_gnn_mlp_b, src, dst), axis=-1)
    return x

_drawn_inputs = setup_inputs


def setup_inputs(seed=0):
    import zlib

    import numpy as np

    out = dict(_drawn_inputs(seed))
    spreads = {'L0_gnn_mb1': (0.0, 0.1),
     'L0_gnn_mb2': (0.0, 0.1),
     'L0_gnn_gb1': (0.0, 2.0),
     'L0_gnn_ub1': (0.0, 0.1),
     'L0_gnn_ub2': (0.0, 0.1),
     'L0_gnn_ln_g': (1.0, 0.2),
     'L0_gnn_ln_b': (0.0, 0.1),
     'L2_gnn_b1': (0.0, 0.1),
     'L2_gnn_b2': (0.0, 0.1),
     'L2_gnn_bn_gamma': (1.0, 0.2),
     'L2_gnn_bn_beta': (0.0, 0.1),
     'L2_gnn_bn_mean': (0.0, 0.1)}
    factors = {'edge_attr_32': 6.119, 'L0_gnn_gW1': 8.0, 'L0_gnn_gW2': 8.0, 'L3_gnn_mlp_b': 27.527}
    for name, (base, spread) in spreads.items():
        noise = np.random.default_rng([zlib.crc32(name.encode()), seed]).standard_normal(out[name].shape)
        drawn = base * np.exp(spread * noise) if base else spread * noise
        out[name] = jnp.asarray(drawn.astype(out[name].dtype))
    for name, factor in factors.items():
        out[name] = (out[name] * factor).astype(out[name].dtype)
    return out
```

```python
import concourse.bass as bass
from concourse import mybir
from contextlib import ExitStack

N = 12500
F = 96
EF = 32
E = 200000
P = 128
EPS = 1e-5

NB = 100
NREAL = -(-N // P)
NPAD = NB * P
BINS = NREAL + 1

TPM = 1568
EPAD = P * TPM
TILES = 1664
assert (E + 127 * NREAL) // P <= TILES and TILES % P == 0 and EPAD - E >= P and TPM % 8 == 0
TCH = TILES // P
TCOL = TILES + 8
HALF = 4
HALVES = TILES // HALF
PAIRS = HALVES // 2
STAGES = HALVES + 2
MW = 98
CH = 4
CHUNKS = NB // CH


def build(nc, a, out):
    f32, i32, bf16 = mybir.dt.float32, mybir.dt.int32, mybir.dt.bfloat16
    ALU = mybir.AluOpType
    ACT = mybir.ActivationFunctionType
    AX = mybir.AxisListType
    DVE = mybir.EngineType.DVE
    SPE = mybir.EngineType.SP
    ds = bass.ds
    ctx = ExitStack()
    with ctx:
        def sb(name, shape, dt=f32):
            return ctx.enter_context(nc.sbuf_tensor(name, shape, dt))

        def sem(name):
            return ctx.enter_context(nc.semaphore(name))

        table0 = nc.dram_tensor("table0", (NPAD, 2 * F), f32).ap()
        table = [None] + [nc.dram_tensor(f"table{i}", (NPAD, F), f32).ap() for i in range(1, 5)]
        rec_dram = nc.dram_tensor("rec_dram", (P * TCOL, 4), f32).ap()
        tile_dram = nc.dram_tensor("tile_dram", (2 * TCH, P), i32).ap()
        tile_dram_s = nc.dram_tensor("tile_dram_s", (TCH, P), i32).ap()

        X = sb("X", [P, NB, F])
        AGG = sb("AGG", [P, NB, MW])
        BIG = sb("BIG", [P, NB * F])
        MD = sb("MD", [P, 3, TCOL])
        tile_row = sb("tile_row", [1, 2 * TILES], i32)
        tile_row_s = tile_row[0:1, TILES:2 * TILES]
        G = sb("G", [P, 8, 2 * F])
        Z = sb("Z", [P, 8, 2 * F])
        H = sb("H", [P, 8, 2 * F + 1])
        M = sb("M", [P, 8, MW])
        S = sb("S", [P, 8, P])
        EA = sb("EA", [EF, 8, P])
        prod = sb("prod", [P, HALF, F])
        idx_st = sb("idx_st", [P, 8], i32)
        rec_st = sb("rec_st", [P, 8, 4])
        glin = sb("glin", [P, 8])
        gth = sb("gth", [P, 8])
        gate = sb("gate", [P, 8])
        iota_row = sb("iota_row", [P, P])
        iota_i = sb("iota_i", [P, P], i32)
        tile_id = sb("tile_id", [P, TCH])
        tile_id_i = sb("tile_id_i", [P, TCH], i32)
        part_i = sb("part_i", [P, P], i32)
        ident = sb("ident", [P, P])
        strict = sb("strict", [P, P])
        ones = sb("ones", [P, P])
        cnt = sb("cnt", [P, BINS])
        row_f = sb("row_f", [P, 6, BINS])
        row_i = sb("row_i", [P, 2, BINS], i32)
        run = sb("run", [P, 2, BINS])
        junk = sb("junk", [P, 2, BINS])
        tcol = sb("tcol", [P, 4, TCH])
        tcol_i = sb("tcol_i", [P, TCH], i32)
        tp_i = sb("tp_i", [2 * TCH, P], i32)
        posf = sb("posf", [P, HALF])
        posi = sb("posi", [P, 3, HALF], i32)
        stat = sb("stat", [P, 3, NB])
        deg = sb("deg", [P, NB])
        dinv = sb("dinv", [P, NB])
        W0 = sb("W0", [F + 1, 2 * F])
        WE = sb("WE", [EF, 2 * F])
        gw2 = sb("gw2", [P, F])
        gb2 = sb("gb2", [P, 1])
        hgb2 = sb("hgb2", [P, 1])
        W2a = sb("W2a", [F + 1, F])
        U1x = sb("U1x", [F, F])
        U1g = sb("U1g", [F, F])
        U2 = sb("U2", [F + 1, F])
        lng = sb("lng", [P, F])
        lnb = sb("lnb", [P, F])
        C1 = sb("C1", [F, F])
        C2 = sb("C2", [F, F])
        b2r = sb("b2r", [P, F])
        L3x = sb("L3x", [F + 1, F])
        L3g = sb("L3g", [F, F])
        vec = sb("vec", [F, 8])
        eps = sb("eps", [P, 1])
        Gf = G[:, :, :].rearrange("p a b -> p (a b)")
        Zf = Z[:, :, :].rearrange("p a b -> p (a b)")
        Hf = H[:, :, :].rearrange("p a b -> p (a b)")
        AS = Gf[:, 0:CH * 97].rearrange("p (k f) -> p k f", k=CH)
        XS = Gf[:, 512:512 + CH * F].rearrange("p (k f) -> p k f", k=CH)
        AT = Zf[0:F + 1, 0:CH * P]
        XT = Zf[0:F + 1, 512:1024]
        GT = Zf[0:F, 1024:1536]
        UT = Hf[0:F + 1, 0:512]
        YT = Hf[0:F, 512:1024]
        pm_dst = BIG[:, 0:TPM].bitcast(i32)
        pm_src = BIG[:, TPM:2 * TPM].bitcast(i32)
        pm_w = BIG[:, 2 * TPM:3 * TPM]
        hi_i = BIG[:, 3 * TPM:4 * TPM].bitcast(i32)
        hi_f = BIG[:, 4 * TPM:5 * TPM]
        hjunk = BIG[:, 5 * TPM:6 * TPM]
        ROWS = BIG[:, 0:3 * TCH * P].rearrange("p (c k e) -> p c k e", k=3, e=P)
        ROWF = BIG[:, 3 * TCH * P:3 * TCH * P + 2 * 2 * P].rearrange("p (c k e) -> p c k e", k=2, e=P)
        AGGf = AGG[:, :, :].rearrange("p b f -> p (b f)")
        REC = AGGf[:, 0:4 * TPM].rearrange("p (t k) -> p t k", k=4)
        MS = BIG[:, 0:4 * TCOL].rearrange("p (t k) -> p t k", k=4)
        TX = BIG[:, :].rearrange("p (b f) -> p b f", f=F)
        Af = AGG[:, :, 0:F]
        T0X = [Zf[0:F + 1, 0:256], Zf[0:F + 1, 256:512]]
        T0S = [Gf[:, 0:384], Gf[:, 384:768]]

        PS = [ctx.enter_context(nc.psum_tensor(f"bank{i}", [P, 512], f32)) for i in range(8)]
        seg_bank = [PS[0], PS[1]]
        z_bank = [[PS[2], PS[3]], [PS[4], PS[5]]]

        s_load = sem("s_load")
        s_pm = sem("s_pm")
        const_ready = sem("const_ready")
        dve_step = sem("dve_step")
        act_step = sem("act_step")
        pool_step = sem("pool_step")
        cnt_ready = sem("cnt_ready")
        tot_ready = sem("tot_ready")
        tiles_known = sem("tiles_known")
        tcol_t = sem("tcol_t")
        trow_out = sem("trow_out")
        s_trow = sem("s_trow")
        s_rows = sem("s_rows")
        rows_f = sem("rows_f")
        rows_t = sem("rows_t")
        md_ready = sem("md_ready")
        s_xt = [sem("s_xt0"), sem("s_xt1")]
        t0_mm = sem("t0_mm")
        t0_ev = sem("t0_ev")
        s_t0 = [sem("s_t00"), sem("s_t01")]
        idx_staged = sem("idx_staged")
        s_g = [[sem(f"s_g{p}_{h}") for h in range(2)] for p in range(5)]
        s_ea = [sem("s_ea0"), sem("s_ea1")]
        z_mm = sem("z_mm")
        z_added = sem("z_added")
        h_ready = sem("h_ready")
        prod_ready = sem("prod_ready")
        lin_ready = sem("lin_ready")
        th_ready = sem("th_ready")
        gate_ready = sem("gate_ready")
        m_ready = sem("m_ready")
        s_ready = sem("s_ready")
        seg_done = sem("seg_done")
        agg_added = sem("agg_added")
        pass_done = sem("pass_done")
        p_staged = sem("p_staged")
        p_tr = sem("p_tr")
        a_ev = sem("a_ev")
        x_ev = sem("x_ev")
        p_gt = sem("p_gt")
        g_ev = sem("g_ev")
        p_u = sem("p_u")
        u_ev = sem("u_ev")
        p_up = sem("p_up")
        h_done = sem("h_done")
        act_sqrt = sem("act_sqrt")
        var_ready = sem("var_ready")
        run_set = sem("run_set")
        pos_got = sem("pos_got")
        pos_ready = sem("pos_ready")
        s_sc = [sem("s_sc0"), sem("s_sc1")]
        s_zero = sem("s_zero")
        rec_built = sem("rec_built")
        s_ms = sem("s_ms")
        x_ready = sem("x_ready")
        agg_zero = sem("agg_zero")
        s_table = sem("s_table")
        s_out = sem("s_out")
        ones_row = sem("ones_row")
        hist_step = sem("hist_step")
        pos_step = sem("pos_step")
        z2_ev = sem("z2_ev")
        rec_staged = sem("rec_staged")
        lk_done = sem("lk_done")
        bn_ready = sem("bn_ready")
        block = ctx.enter_context(nc.Block())

        def chain(eng, semaphore):
            count = [0]

            def step(ins):
                count[0] += 1
                ins.then_inc(semaphore, 1)
                eng.wait_ge(semaphore, count[0])
            return step

        def node_rows(ap):
            return ap.rearrange("(b p) f -> p b f", p=P)

        def meta(p, k, t0, n):
            if p == 1:
                return MS[:, ds(t0, n), k]
            return MD[:, k, ds(t0, n)]

        WEIGHTED = (False, True, False, False, True)

        @block.sync
        def _(sp):
            full = N // P
            sp.dma_start(pm_dst, a["dst"].rearrange("(p t) -> p t", p=P)).then_inc(s_pm, 16)
            loads = [
                (X[:, 0:full, :], node_rows(a["x"][0:full * P, :])),
                (W0[0:F, 0:F], a["gW1"][0:F, :]), (W0[0:F, F:2 * F], a["mW1"][0:F, :]),
                (W0[F:F + 1, 0:F], a["gb1"].unsqueeze(0)), (W0[F:F + 1, F:2 * F], a["mb1"].unsqueeze(0)),
                (WE[:, 0:F], a["gW1"][F:F + EF, :]), (WE[:, F:2 * F], a["mW1"][F:F + EF, :]),
                (gw2[:, :], a["gW2"].rearrange("f a -> (a f)").partition_broadcast(P)),
                (gb2[:, :], a["gb2"].partition_broadcast(P)),
                (W2a[0:F, :], a["mW2"]), (W2a[F:F + 1, :], a["mb2"].unsqueeze(0)),
                (U1x[:, :], a["uW1"][0:F, :]), (U1g[:, :], a["uW1"][F:2 * F, :]),
                (U2[0:F, :], a["uW2"]), (U2[F:F + 1, :], a["ub2"].unsqueeze(0)),
                (lng[:, :], a["ln_g"].partition_broadcast(P)), (lnb[:, :], a["ln_b"].partition_broadcast(P)),
                (C1[:, :], a["W1"]), (C2[:, :], a["W2"]), (b2r[:, :], a["b2"].partition_broadcast(P)),
                (L3x[0:F, :], a["mlp_wT"][0:F, :]), (L3x[F:F + 1, :], a["mlp_b"].unsqueeze(0)),
                (L3g[:, :], a["mlp_wT"][F:2 * F, :]),
            ] + [(vec[:, i:i + 1], a[n].unsqueeze(1)) for i, n in enumerate(("ub1", "b1", "bn_gamma", "bn_beta", "bn_mean", "bn_var"))]
            sp.wait_ge(const_ready, 1)
            for o, i in loads:
                sp.dma_start(o, i).then_inc(s_load, 16)
            sp.dma_start(X[0:N - full * P, full, :], a["x"][full * P:N, :]).then_inc(s_load, 16)
            assert len(loads) + 1 == 30, len(loads)
            with sp.Fori(0, NB // 4) as i:
                for h in range(2):
                    sp.wait_ge(t0_mm, i * 2 + h + 1)
                    sp.nop(nofuse=True)
                    sp.dma_start(T0X[h][0:F, :], a["xT"][:, ds(i * 512 + h * 256, 256)]).then_inc(s_xt[h], 16)
            sp.wait_ge(const_ready, 8)
            sp.dma_start(rec_dram.rearrange("(p t) k -> p (t k)", p=P), AGGf[:, 0:4 * TCOL]).then_inc(s_zero, 16)
            sp.wait_ge(trow_out, 1)
            sp.dma_start(tile_dram, tp_i[:, :]).then_inc(s_trow, 16)
            sp.wait_ge(s_trow, 16)
            sp.dma_start(tile_row[0:1, :], tile_dram.rearrange("(o c) p -> o (c p)", o=1)).then_inc(s_trow, 16)
            sp.wait_ge(s_trow, 32)
            with sp.Fori(0, PAIRS) as i:
                _, first = nc.values_load_multi_w_load_instructions(
                    tile_row[0:1, ds(i * 8 + TILES, 8)], engines=[SPE], min_val=0, max_val=EPAD - P,
                    skip_runtime_bounds_check_because="DVE clamps the first edge to EPAD - 128")
                for h in range(2):
                    sp.wait_ge(z_mm, i * 2 + h + 1)
                    sp.nop(nofuse=True)
                    for u in range(HALF):
                        sp.dma_start(EA[:, HALF * h + u, :], a["eaT"][:, ds(first[HALF * h + u], P)]).then_inc(s_ea[h], 16)
            sp.wait_ge(x_ready, 1)
            sp.dma_start(node_rows(table[1]), X[:, :, :]).then_inc(s_table, 16)
            sp.dma_start(pm_dst, a["dst"].rearrange("(p t) -> p t", p=P)).then_inc(s_pm, 16)
            sp.dma_start(pm_src, a["src"].rearrange("(p t) -> p t", p=P)).then_inc(s_pm, 16)
            sp.dma_start(pm_w, a["w"].rearrange("(p t) -> p t", p=P)).then_inc(s_pm, 16)
            sp.wait_ge(trow_out, 2)
            sp.dma_start(tile_dram_s, tp_i[0:TCH, :]).then_inc(s_trow, 16)
            sp.wait_ge(s_trow, 48)
            sp.dma_start(tile_row_s, tile_dram_s.rearrange("(o c) p -> o (c p)", o=1)).then_inc(s_trow, 16)
            for h in range(2):
                sp.wait_ge(s_sc[h], 64 * (TPM // 8))
            sp.dma_start(MS.rearrange("p t k -> p (t k)"), rec_dram.rearrange("(p t) k -> p (t k)", p=P)).then_inc(s_ms, 16)
            sp.wait_ge(x_ready, 2)
            sp.dma_start(node_rows(table[2]), TX).then_inc(s_table, 16)
            sp.wait_ge(x_ready, 3)
            sp.dma_start(node_rows(table[3]), TX).then_inc(s_table, 16)
            sp.wait_ge(x_ready, 4)
            sp.dma_start(node_rows(table[4]), X[:, :, :]).then_inc(s_table, 16)
            sp.wait_ge(x_ready, 5)
            sp.dma_start(node_rows(out[0:full * P, :]), X[:, 0:full, :]).then_inc(s_out, 16)
            sp.dma_start(out[full * P:N, :], X[0:N - full * P, full, :]).then_inc(s_out, 16)
            sp.wait_ge(s_out, 32)

        @block.gpsimd
        def _(pool):
            step = chain(pool, pool_step)
            pool.memset(X[:, N // P:NB, :], 0.0).then_inc(const_ready, 1)
            pool.iota(iota_i[:, :], pattern=[[1, P]], base=0, channel_multiplier=0).then_inc(const_ready, 1)
            pool.iota(part_i[:, :], pattern=[[0, P]], base=0, channel_multiplier=1).then_inc(const_ready, 1)
            pool.iota(tile_id_i[:, :], pattern=[[P, TCH]], base=0, channel_multiplier=1).then_inc(const_ready, 1)
            pool.memset(ones[:, :], 1.0).then_inc(const_ready, 1)
            pool.memset(H[:, :, 2 * F:2 * F + 1], 1.0).then_inc(const_ready, 1)
            pool.memset(M[:, :, MW - 1:MW], 1.0).then_inc(const_ready, 1)
            pool.memset(AGG[:, :, :], 0.0).then_inc(const_ready, 1)
            pool.memset(MD[:, :, TILES:TCOL], 0.0).then_inc(const_ready, 1)
            pool.memset(eps[:, :], EPS).then_inc(const_ready, 1)
            pool.wait_ge(tiles_known, 1)
            pool.nop(nofuse=True)
            for c in range(TCH):
                for k, n in enumerate(("src", "dst", "w")):
                    o = ROWS[:, c, k, :] if k == 2 else ROWS[:, c, k, :].bitcast(i32)
                    pool.indirect_dma_start(out=o, out_offset=None, in_=a[n].rearrange("(n a) -> n a", a=1),
                                            in_offset=bass.IndirectOffsetOnAxis(ap=tcol_i[:, c:c + 1], axis=0)).then_inc(s_rows, 16)

            def gathers(p, src_table, width):
                with pool.Fori(0, PAIRS) as i:
                    for h in range(2):
                        pool.wait_ge(idx_staged, i * 2 + (STAGES * p + h + 1))
                        if p == 0:
                            pool.wait_ge(z_added, i * 2 + h + 1)
                        else:
                            pool.wait_ge(seg_done, i * 2 + (HALVES * p + h + 1))
                        pool.nop(nofuse=True)
                        for u in range(HALF * h, HALF * h + HALF):
                            pool.indirect_dma_start(
                                out=G[:, u, 0:width], out_offset=None, in_=src_table,
                                in_offset=bass.IndirectOffsetOnAxis(ap=idx_st[:, u:u + 1], axis=0)).then_inc(s_g[p][h], 16)

            def stage(c, first, x_too, width):
                pool.wait_ge(p_tr, c + first + 1)
                pool.tensor_copy(AS[:, :, 0:width], AGG[:, ds(c * CH, CH), 0:width]).then_inc(p_staged, 1)
                if x_too:
                    pool.tensor_copy(XS[:, :, :], X[:, ds(c * CH, CH), :]).then_inc(p_staged, 1)

            for h in range(2):
                pool.wait_ge(s_t0[h], 16 * (NB // 4))
            pool.wait_ge(t0_mm, NB // 2 + 2)
            gathers(0, table0, 2 * F)
            pool.wait_ge(pass_done, 1)
            with pool.Fori(0, CHUNKS) as c:
                stage(c, 0, True, 97)
            with pool.Fori(0, TPM // 8) as i:
                for h in range(2):
                    pool.wait_ge(pos_ready, i * 2 + h + 1)
                    pool.wait_ge(rec_staged, i * 2 + h + 1)
                    pool.nop(nofuse=True)
                    for u in range(HALF * h, HALF * h + HALF):
                        pool.indirect_dma_start(
                            out=rec_dram, out_offset=bass.IndirectOffsetOnAxis(ap=idx_st[:, u:u + 1], axis=0),
                            in_=rec_st[:, u, :], in_offset=None).then_inc(s_sc[h], 16)
            for h in range(2):
                pool.wait_ge(s_sc[h], 64 * (TPM // 8))
            for p in range(1, 5):
                if p > 1:
                    pool.wait_ge(x_ready, p)
                pool.memset(AGG[:, :, :], 0.0).then_inc(agg_zero, 1)
                pool.wait_ge(s_table, 16 * p)
                gathers(p, table[p], F)
                pool.wait_ge(pass_done, p + 1)
                if p == 2:
                    with pool.Fori(0, CHUNKS) as c:
                        stage(c, CHUNKS, False, F)
                if p == 4:
                    with pool.Fori(0, CHUNKS) as c:
                        stage(c, 2 * CHUNKS, True, F)

        @block.tensor
        def _(pe):
            mm = nc.tensor.matmul
            pe.sem_inc(t0_mm, 2)
            pe.sem_inc(seg_done, 2)
            pe.sem_inc(z_mm, 2)
            for s in (p_tr, p_gt, p_u, p_up):
                pe.sem_inc(s, 1)
            pe.wait_ge(s_load, 16 * 30)
            pe.wait_ge(ones_row, 1)
            with pe.Fori(0, NB // 4) as i:
                for h in range(2):
                    pe.wait_ge(s_xt[h], i * 16 + 16)
                    pe.wait_ge(t0_ev, i * 2 + h + 1)
                    for k in range(2):
                        last = mm(z_bank[0][h][:, k * 192:(k + 1) * 192], T0X[h][:, k * P:(k + 1) * P], W0[:, :], start=True, stop=True)
                    last.then_inc(t0_mm, 1)

            def totals(n):
                pe.wait_ge(cnt_ready, n)
                mm(PS[6][:, 0:BINS], ones[:, :], cnt[:, :], start=True, stop=True).then_inc(tot_ready, 1)

            def tile_rows(n):
                pe.wait_ge(tiles_known, n)
                k = 2 * TCH if n == 1 else TCH
                nc.tensor.transpose(PS[7][0:k, 0:P], tcol[:, 0:2, :].rearrange("p a c -> p (a c)")[:, 0:k], ident[:, :]).then_inc(tcol_t, 1)

            totals(1)
            tile_rows(1)
            for c in range(TCH):
                pe.wait_ge(rows_f, c + 1)
                if c >= 2:
                    pe.wait_ge(md_ready, c - 1)
                for k in range(3):
                    src = ROWS[:, c, 2, :] if k == 2 else ROWF[:, c % 2, k, :]
                    last = nc.tensor.transpose(seg_bank[c % 2][:, k * P:(k + 1) * P], src, ident[:, :])
                last.then_inc(rows_t, 1)

            def z_half(i, h):
                pe.wait_ge(s_ea[h], i * 64 + 64)
                pe.wait_ge(z_added, i * 2 + h + 1)
                for u in range(HALF):
                    last = mm(z_bank[h][u // 2][:, (u % 2) * 192:(u % 2) * 192 + 192], EA[:, HALF * h + u, :], WE[:, :], start=True, stop=True)
                last.then_inc(z_mm, 1)

            def seg_half(p, i, h, width):
                if p == 0:
                    pe.wait_ge(m_ready, i * 2 + h + 1)
                else:
                    pe.wait_ge(s_g[p][h], i * 64 + 64)
                pe.wait_ge(s_ready, i * 2 + (HALVES * p + h + 1))
                pe.wait_ge(agg_added, i * 8 + (TILES * p + 4 * h + 4))
                for u in range(HALF):
                    rhs = M[:, HALF * h + u, :] if p == 0 else G[:, HALF * h + u, 0:F]
                    last = mm(seg_bank[h][:, u * P:u * P + width], S[:, HALF * h + u, :], rhs, start=True, stop=True)
                last.then_inc(seg_done, 1)

            pe.wait_ge(md_ready, TCH)
            pe.wait_ge(t0_ev, NB // 2 + 2)
            z_half(0, 0)
            with pe.Fori(0, PAIRS - 1) as i:
                z_half(i, 1)
                seg_half(0, i, 0, MW)
                z_half(i + 1, 0)
                seg_half(0, i, 1, MW)
            z_half(PAIRS - 1, 1)
            seg_half(0, PAIRS - 1, 0, MW)
            seg_half(0, PAIRS - 1, 1, MW)

            def transposes(c, first, staged0, staged, width, x_too):
                pe.wait_ge(p_staged, c * staged + (staged0 + staged))
                pe.wait_ge(a_ev, c + first + 1)
                pe.wait_ge(x_ev, c + min(first, CHUNKS) + 1) if x_too else None
                for k in range(CH):
                    last = nc.tensor.transpose(PS[2][0:width, k * P:(k + 1) * P], AS[:, k, 0:width], ident[:, :])
                if x_too:
                    for k in range(CH):
                        last = nc.tensor.transpose(PS[3][0:F, k * P:(k + 1) * P], XS[:, k, :], ident[:, :])
                last.then_inc(p_tr, 1)

            pe.wait_ge(ones_row, 2)
            with pe.Fori(0, CHUNKS) as c:
                transposes(c, 0, 0, 2, 97, True)
                pe.wait_ge(a_ev, c + 2)
                pe.wait_ge(g_ev, c + 1)
                mm(PS[4][0:F, :], W2a[:, :], AT, start=True, stop=True).then_inc(p_gt, 1)
                pe.wait_ge(g_ev, c + 2)
                pe.wait_ge(x_ev, c + 2)
                pe.wait_ge(u_ev, c + 1)
                mm(PS[5][0:F, :], U1x[:, :], XT[0:F, :], start=True, stop=False)
                mm(PS[5][0:F, :], U1g[:, :], GT, start=False, stop=True).then_inc(p_u, 1)
                pe.wait_ge(u_ev, c + 2)
                pe.wait_ge(h_done, c + 1)
                for k in range(CH):
                    last = mm(PS[6][:, k * F:(k + 1) * F], UT[:, k * P:(k + 1) * P], U2[:, :], start=True, stop=True)
                last.then_inc(p_up, 1)
            totals(2)
            mm(PS[5][:, 0:BINS], strict[:, :], cnt[:, :], start=True, stop=True).then_inc(tot_ready, 1)
            tile_rows(2)

            def agg_pass(p):
                with pe.Fori(0, PAIRS) as i:
                    for h in range(2):
                        seg_half(p, i, h, F)

            agg_pass(1)
            agg_pass(2)
            with pe.Fori(0, CHUNKS) as c:
                transposes(c, CHUNKS, 2 * CHUNKS, 1, F, False)
                pe.wait_ge(a_ev, c + CHUNKS + 2)
                pe.wait_ge(z2_ev, c + 1)
                mm(PS[4][0:F, :], C1[:, :], AT[0:F, :], start=True, stop=True).then_inc(p_gt, 1)
                pe.wait_ge(bn_ready, c + 2)
                pe.wait_ge(h_done, c + CHUNKS + 1)
                for k in range(CH):
                    last = mm(PS[6][:, k * F:(k + 1) * F], YT[:, k * P:(k + 1) * P], C2[:, :], start=True, stop=True)
                last.then_inc(p_up, 1)
            agg_pass(3)
            agg_pass(4)
            pe.wait_ge(ones_row, 3)
            with pe.Fori(0, CHUNKS) as c:
                transposes(c, 2 * CHUNKS, 3 * CHUNKS, 2, F, True)
                pe.wait_ge(a_ev, c + 2 * CHUNKS + 2)
                pe.wait_ge(x_ev, c + CHUNKS + 2)
                pe.wait_ge(h_done, c + 2 * CHUNKS + 1)
                for k in range(CH):
                    mm(PS[6][:, k * F:(k + 1) * F], XT[:, k * P:(k + 1) * P], L3x[:, :], start=True, stop=False)
                    last = mm(PS[6][:, k * F:(k + 1) * F], AT[0:F, k * P:(k + 1) * P], L3g[:, :], start=False, stop=True)
                last.then_inc(p_up, 1)

        @block.scalar
        def _(act):
            step = chain(act, act_step)
            act_fn = nc.scalar.activation
            act.sem_inc(t0_ev, 2)
            act.sem_inc(a_ev, 1)
            act.sem_inc(u_ev, 1)
            act.sem_inc(z2_ev, 1)

            def t0_half(i, h, again):
                act.wait_ge(t0_mm, i * 2 + h + 3)
                if again:
                    act.wait_ge(s_t0[h], i * 16)
                act_fn(T0S[h], z_bank[0][h][:, 0:384], ACT.Copy).then_inc(t0_ev, 1)
                act.wait_ge(t0_ev, i * 2 + h + 3)
                act.dma_start(table0[ds(i * 512 + h * 256, 256), :].rearrange("(k p) f -> p k f", p=P),
                              T0S[h].rearrange("p (k f) -> p k f", k=2)).then_inc(s_t0[h], 16)

            for h in range(2):
                t0_half(0, h, False)
            with act.Fori(1, NB // 4) as i:
                for h in range(2):
                    t0_half(i, h, True)
            step(act_fn(hgb2[:, :], gb2[:, :], ACT.Copy, scale=0.5))

            def stage(p, i, h):
                act.wait_ge(idx_staged, i * 2 + (STAGES * p + h)) if not (p == 0 and isinstance(i, int) and i == 0) else None
                act_fn(idx_st[:, HALF * h:HALF * h + HALF], meta(p, 0, i * 8 + HALF * h, HALF), ACT.Copy).then_inc(idx_staged, 1)

            def gelu(i, h):
                act.wait_ge(z_added, i * 2 + h + 3)
                act.wait_ge(m_ready, i * 2 + h - 1) if not isinstance(i, int) else None
                act_fn(H[:, HALF * h:HALF * h + HALF, 0:2 * F], Z[:, HALF * h:HALF * h + HALF, :], ACT.Gelu).then_inc(h_ready, 1)

            def tanh(i, h):
                act.wait_ge(lin_ready, i * 2 + h + 1)
                act_fn(gth[:, HALF * h:HALF * h + HALF], glin[:, HALF * h:HALF * h + HALF], ACT.Tanh, bias=hgb2[:, :], scale=0.5).then_inc(th_ready, 1)

            act.wait_ge(md_ready, TCH)
            stage(0, 0, 0)
            act.wait_ge(idx_staged, 1)
            act_fn(idx_st[:, HALF:2 * HALF], meta(0, 0, HALF, HALF), ACT.Copy).then_inc(idx_staged, 1)
            gelu(0, 0)
            stage(0, 1, 0)
            gelu(0, 1)
            stage(0, 1, 1)
            tanh(0, 0)
            with act.Fori(1, PAIRS) as i:
                gelu(i, 0)
                stage(0, i + 1, 0)
                tanh(i - 1, 1)
                gelu(i, 1)
                stage(0, i + 1, 1)
                tanh(i, 0)
            tanh(PAIRS - 1, 1)

            with act.Fori(0, CHUNKS) as c:
                act.wait_ge(p_tr, c + 2)
                act.wait_ge(p_gt, c + 1)
                act_fn(AT, PS[2][0:F + 1, :], ACT.Copy).then_inc(a_ev, 1)
                act.wait_ge(p_u, c + 2)
                act.wait_ge(p_up, c + 1)
                act_fn(UT[0:F, :], PS[5][0:F, :], ACT.Gelu, bias=vec[:, 0:1]).then_inc(u_ev, 1)

            sqrts = [0]

            def sqrt(o, i, scale, bias):
                sqrts[0] += 1
                act.wait_ge(var_ready, sqrts[0])
                act_fn(o, i, ACT.Sqrt, bias=bias, scale=scale).then_inc(act_sqrt, 1)

            def ln_sqrt():
                sqrt(stat[:, 2, :], stat[:, 1, :], 1.0 / F, eps[:, :])

            ln_sqrt()
            ln_sqrt()

            def stage_records(i, h):
                act_fn(rec_st[:, HALF * h:HALF * h + HALF, :], REC[:, ds(i * 8 + HALF * h, HALF), :], ACT.Copy).then_inc(rec_staged, 1)

            act.wait_ge(run_set, 1)
            for h in range(2):
                stage_records(0, h)
            with act.Fori(1, TPM // 8) as i:
                for h in range(2):
                    act.wait_ge(s_sc[h], i * 64)
                    stage_records(i, h)
            act.wait_ge(s_ms, 16)

            def stagings(p):
                act.wait_ge(idx_staged, STAGES * p)
                for h in range(2):
                    act.wait_ge(idx_staged, STAGES * p + h)
                    act_fn(idx_st[:, HALF * h:HALF * h + HALF], meta(p, 0, HALF * h, HALF), ACT.Copy).then_inc(idx_staged, 1)
                with act.Fori(0, PAIRS) as i:
                    for h in range(2):
                        act.wait_ge(s_g[p][h], i * 64 + 64)
                        stage(p, i + 1, h)

            stagings(1)
            ln_sqrt()
            sqrt(stat[:, 2, :], deg[:, :], 1.0, 0.0)
            sqrt(vec[:, 6:7], vec[:, 5:6], 1.0, eps[0:F, :])
            stagings(2)
            with act.Fori(0, CHUNKS) as c:
                act.wait_ge(p_tr, c + CHUNKS + 2)
                act.wait_ge(p_gt, c + CHUNKS + 1)
                act_fn(AT[0:F, :], PS[2][0:F, :], ACT.Copy).then_inc(a_ev, 1)
                act.wait_ge(p_gt, c + CHUNKS + 2)
                act.wait_ge(lk_done, c + 1)
                act_fn(GT, PS[4][0:F, :], ACT.Identity, bias=vec[:, 1:2]).then_inc(z2_ev, 1)
            stagings(3)
            ln_sqrt()
            stagings(4)
            with act.Fori(0, CHUNKS) as c:
                act.wait_ge(p_tr, c + 2 * CHUNKS + 2)
                act.wait_ge(p_up, c + 2 * CHUNKS + 1)
                act_fn(AT[0:F, :], PS[2][0:F, :], ACT.Copy).then_inc(a_ev, 1)
            ln_sqrt()

        @block.vector
        def _(dve):
            step = chain(dve, dve_step)
            v = nc.vector
            dve.sem_inc(z_added, 2)
            dve.sem_inc(agg_added, 8)
            for s in (x_ev, g_ev, h_done, lk_done, bn_ready):
                dve.sem_inc(s, 1)
            v.memset(Zf[F:F + 1, 0:512], 1.0).then_inc(ones_row, 1)
            dve.wait_ge(const_ready, 10)
            step(v.tensor_copy(iota_row[:, :], iota_i[:, :]))
            step(v.tensor_copy(tile_id[:, :], tile_id_i[:, :]))
            step(v.tensor_tensor(ident[:, :], iota_i[:, :], part_i[:, :], ALU.is_equal))
            step(v.tensor_tensor(strict[:, :], iota_i[:, :], part_i[:, :], ALU.is_gt))

            def histogram(key, n):
                step(v.tensor_single_scalar(hi_i, key, 7, ALU.logical_shift_right))
                step(v.tensor_copy(hi_f, hi_i))
                with dve.Fori(0, BINS) as b:
                    v.tensor_scalar(hjunk, hi_f, iota_row[:, ds(b, 1)], None, ALU.is_equal, ALU.add,
                                    accum_out=cnt[:, ds(b, 1)]).then_inc(hist_step, 1)
                    dve.wait_ge(hist_step, b + (BINS * (n - 1) + 1))
                dve.engine_nop().then_inc(cnt_ready, 1)

            COUNT, NTILE, TINCL, DG, TEXCL, ONE = range(6)

            def tiles_of(n):
                c, nt, ti, dg, te, one = (row_f[:, k, :] for k in (COUNT, NTILE, TINCL, DG, TEXCL, ONE))
                step(v.memset(one, 1.0))
                dve.wait_ge(tot_ready, 1 if n == 1 else 3)
                step(v.tensor_copy(c, PS[6][:, 0:BINS]))
                step(v.memset(c[:, NREAL:BINS], 0.0))
                step(v.tensor_scalar(row_i[:, 0, :], c, 127.0, None, ALU.add))
                step(v.tensor_single_scalar(row_i[:, 1, :], row_i[:, 0, :], 7, ALU.logical_shift_right))
                step(v.tensor_copy(nt, row_i[:, 1, :]))
                step(v.tensor_tensor_scan(ti, one, nt, 0.0, ALU.mult, ALU.add))
                step(v.tensor_tensor(te, ti, nt, ALU.subtract))
                step(v.scalar_tensor_tensor(dg, nt, -128.0, c, ALU.mult, ALU.add))
                for k in range(TCH):
                    step(v.tensor_scalar(junk[:, 0, :], ti, tile_id[:, k:k + 1], None, ALU.is_le, ALU.add,
                                         accum_out=tcol[:, 0, k:k + 1]))
                    if n == 1:
                        step(v.scalar_tensor_tensor(junk[:, 1, :], ti, tile_id[:, k:k + 1], dg, ALU.is_le, ALU.mult,
                                                    accum_out=tcol[:, 1, k:k + 1]))
                step(v.tensor_scalar(tcol[:, 0, :], tcol[:, 0, :], float(NREAL), None, ALU.min))
                if n == 1:
                    step(v.scalar_tensor_tensor(tcol[:, 1, :], tile_id[:, :], 128.0, tcol[:, 1, :], ALU.mult, ALU.add))
                    step(v.tensor_scalar(tcol[:, 1, :], tcol[:, 1, :], float(EPAD - P), None, ALU.min))
                    step(v.tensor_scalar(tcol[:, 2, :], tcol[:, 0, :], 128.0, None, ALU.mult))
                    step(v.tensor_copy(tcol_i[:, :], tcol[:, 1, :]))
                dve.engine_nop().then_inc(tiles_known, 1)
                dve.wait_ge(tcol_t, n)
                k = 2 * TCH if n == 1 else TCH
                step(v.tensor_copy(tp_i[0:k, :], PS[7][0:k, 0:P]))
                dve.engine_nop().then_inc(trow_out, 1)

            dve.wait_ge(s_pm, 16)
            histogram(pm_dst, 1)
            tiles_of(1)
            dve.wait_ge(s_rows, 16 * 3 * TCH)
            for c in range(TCH):
                if c >= 2:
                    dve.wait_ge(rows_t, c - 1)
                step(v.tensor_scalar(ROWF[:, c % 2, 0, :], ROWS[:, c, 0, :].bitcast(i32), float(NPAD - 1), None, ALU.min))
                v.tensor_scalar(ROWF[:, c % 2, 1, :], ROWS[:, c, 1, :].bitcast(i32), tcol[:, 2, c:c + 1], None,
                                ALU.subtract).then_inc(rows_f, 1)
                if c >= 1:
                    dve.wait_ge(rows_t, c)
                    v.tensor_copy(MD[:, :, (c - 1) * P:c * P], seg_bank[(c - 1) % 2][:, 0:3 * P].rearrange("p (k e) -> p k e", k=3)).then_inc(md_ready, 1)
            dve.wait_ge(rows_t, TCH)
            v.tensor_copy(MD[:, :, (TCH - 1) * P:TCH * P], seg_bank[(TCH - 1) % 2][:, 0:3 * P].rearrange("p (k e) -> p k e", k=3)).then_inc(md_ready, 1)
            dve.wait_ge(md_ready, TCH)
            dve.wait_ge(s_trow, 32)
            dve.wait_ge(s_zero, 16)

            def blocks(p, col):
                row = tile_row_s if p == 1 else tile_row
                _, b = nc.values_load_multi_w_load_instructions(
                    row[0:1, ds(col, 8)] if p != 1 else tile_row[0:1, ds(col + TILES, 8)], engines=[DVE], min_val=0, max_val=NREAL,
                    skip_runtime_bounds_check_because="the block of a tile is clamped to NREAL when it is computed")
                return b

            def one_hot(p, i, h, u):
                slot = HALF * h + u
                lo = meta(p, 1, i * 8 + slot, 1)
                if WEIGHTED[p]:
                    ins = v.tensor_scalar(S[:, slot, :], iota_row[:, :], lo, meta(p, 2, i * 8 + slot, 1), ALU.is_equal, ALU.mult)
                else:
                    ins = v.tensor_scalar(S[:, slot, :], iota_row[:, :], lo, None, ALU.is_equal)
                if u == HALF - 1:
                    ins.then_inc(s_ready, 1)

            def add(p, i, h, u, b, width):
                dve.wait_ge(agg_added, i * 8 + (TILES * p + HALF * h + u + 8))
                v.tensor_tensor(AGG[:, ds(b[HALF * h + u], 1), 0:width].rearrange("p b f -> p (b f)"),
                                AGG[:, ds(b[HALF * h + u], 1), 0:width].rearrange("p b f -> p (b f)"),
                                seg_bank[h][:, u * P:u * P + width], ALU.add).then_inc(agg_added, 1)

            def hots_and_adds(p, hot, add_, b, width):
                if hot:
                    dve.wait_ge(seg_done, hot[0] * 2 + (HALVES * p + hot[1] + 1))
                if add_:
                    dve.wait_ge(seg_done, add_[0] * 2 + (HALVES * p + add_[1] + 3))
                for u in range(HALF):
                    if add_:
                        add(p, add_[0], add_[1], u, b, width)
                    if hot:
                        one_hot(p, hot[0], hot[1], u)

            def z_add(i, h):
                dve.wait_ge(s_g[0][h], i * 64 + 64)
                dve.wait_ge(z_mm, i * 2 + h + 3)
                if not isinstance(i, int):
                    dve.wait_ge(h_ready, i * 2 + h - 1)
                for k in range(2):
                    sl = slice(HALF * h + 2 * k, HALF * h + 2 * k + 2)
                    last = v.tensor_tensor(Z[:, sl, :], G[:, sl, :], z_bank[h][k][:, 0:384].rearrange("p (t f) -> p t f", t=2), ALU.add)
                last.then_inc(z_added, 1)

            def gate_lin(i, h):
                dve.wait_ge(h_ready, i * 2 + h + 1)
                sl = slice(HALF * h, HALF * h + HALF)
                if not (isinstance(i, int) and i == 0 and h == 0):
                    dve.wait_ge(lin_ready, i * 2 + h)
                v.tensor_tensor(prod[:, :, :], H[:, sl, 0:F], gw2[:, :].unsqueeze(1).to_broadcast([P, HALF, F]), ALU.mult).then_inc(prod_ready, 1)
                dve.wait_ge(prod_ready, i * 2 + h + 1)
                v.reduce_sum(glin[:, sl], prod[:, :, :], axis=AX.X).then_inc(lin_ready, 1)

            def gated(i, h):
                dve.wait_ge(th_ready, i * 2 + h + 1)
                sl = slice(HALF * h, HALF * h + HALF)
                v.tensor_scalar(gate[:, sl], gth[:, sl], 0.5, 0.5, ALU.mult, ALU.add).then_inc(gate_ready, 1)
                dve.wait_ge(gate_ready, i * 2 + h + 1)
                dve.wait_ge(seg_done, i * 2 + h + 1)
                v.tensor_tensor(M[:, sl, 0:F + 1], H[:, sl, F:2 * F + 1],
                                gate[:, sl].unsqueeze(2).to_broadcast([P, HALF, F + 1]), ALU.mult).then_inc(m_ready, 1)

            z_add(0, 0)
            z_add(0, 1)
            gate_lin(0, 0)
            hots_and_adds(0, (0, 0), None, None, MW)
            gated(0, 0)
            with dve.Fori(1, PAIRS) as i:
                b = blocks(0, i * 8 - 8)
                z_add(i, 0)
                gate_lin(i - 1, 1)
                hots_and_adds(0, (i - 1, 1), (i - 1, 0), b, MW)
                gated(i - 1, 1)
                z_add(i, 1)
                gate_lin(i, 0)
                hots_and_adds(0, (i, 0), (i - 1, 1), b, MW)
                gated(i, 0)
            L = PAIRS - 1
            gate_lin(L, 1)
            b = blocks(0, L * 8)
            hots_and_adds(0, (L, 1), (L, 0), b, MW)
            gated(L, 1)
            hots_and_adds(0, None, (L, 1), b, MW)
            dve.wait_ge(agg_added, TILES + 8)
            dve.wait_ge(th_ready, HALVES)
            v.memset(Hf[F:F + 1, 0:512], 1.0).then_inc(ones_row, 1)
            step(v.tensor_scalar(deg[:, :], AGG[:, :, MW - 1:MW].rearrange("p b f -> p (b f)"), 1.0, None, ALU.add))
            dve.engine_nop().then_inc(pass_done, 1)

            with dve.Fori(0, CHUNKS) as c:
                dve.wait_ge(p_tr, c + 2)
                dve.wait_ge(p_u, c + 1)
                v.tensor_copy(XT[0:F, :], PS[3][0:F, :]).then_inc(x_ev, 1)
                dve.wait_ge(p_gt, c + 2)
                v.tensor_copy(GT, PS[4][0:F, :]).then_inc(g_ev, 1)
                dve.wait_ge(p_up, c + 2)
                v.tensor_tensor(AGG[:, ds(c * CH, CH), 0:F], X[:, ds(c * CH, CH), :],
                                PS[6][:, 0:CH * F].rearrange("p (k f) -> p k f", k=CH), ALU.add).then_inc(h_done, 1)
            dve.wait_ge(h_done, CHUNKS + 1)

            sqrts = [0]

            def root():
                sqrts[0] += 1
                dve.engine_nop().then_inc(var_ready, 1)
                dve.wait_ge(act_sqrt, sqrts[0])

            def wide(x):
                return x.unsqueeze(2).to_broadcast([P, NB, F])

            def per_feature(x):
                return x.unsqueeze(1).to_broadcast([P, NB, F])

            def layernorm(Y, square):
                mean, var, std = stat[:, 0, :], stat[:, 1, :], stat[:, 2, :]
                step(v.reduce_sum(mean, Y, axis=AX.X))
                step(v.tensor_scalar(mean, mean, 1.0 / F, None, ALU.mult))
                step(v.tensor_tensor(Y, Y, wide(mean), ALU.subtract))
                step(v.tensor_tensor(square, Y, Y, ALU.mult))
                step(v.reduce_sum(var, square, axis=AX.X))
                root()
                step(v.reciprocal(std, std))
                step(v.tensor_tensor(Y, Y, wide(std), ALU.mult))

            Xa = X[:, :, :]
            layernorm(Af, TX)
            step(v.tensor_tensor(Af, Af, per_feature(lng[:, :]), ALU.mult))
            step(v.tensor_tensor(Af, Af, per_feature(lnb[:, :]), ALU.add))
            step(v.tensor_tensor(Xa, Xa, Af, ALU.add))
            layernorm(Xa, TX)
            dve.engine_nop().then_inc(x_ready, 1)

            dve.wait_ge(s_pm, 64)
            histogram(pm_src, 2)
            tiles_of(2)
            step(v.scalar_tensor_tensor(run[:, 0, :], row_f[:, TEXCL, :], 128.0, PS[5][:, 0:BINS], ALU.mult, ALU.add))
            step(v.tensor_scalar(run[:, 0, NREAL:BINS], PS[5][:, NREAL:BINS], float(P * TILES), None, ALU.add))
            step(v.tensor_copy(REC[:, :, 0], pm_dst))
            step(v.tensor_single_scalar(hi_i, pm_src, 127, ALU.bitwise_and))
            step(v.tensor_copy(REC[:, :, 1], hi_i))
            step(v.tensor_copy(REC[:, :, 2], pm_w))
            step(v.memset(REC[:, :, 3], 0.0))
            dve.engine_nop().then_inc(run_set, 1)
            dve.engine_nop().then_inc(pos_got, 1)

            def positions(i, h, first):
                for u in range(HALF):
                    t = i * 8 + HALF * h + u
                    a_, b_ = u % 2, (u + 1) % 2
                    key = hi_f[:, ds(t, 1)]
                    dve.wait_ge(run_set, t + 1)
                    dve.wait_ge(pos_got, t + 1)
                    v.scalar_tensor_tensor(run[:, b_, :], iota_row[:, 0:BINS], key, run[:, a_, :], ALU.is_equal, ALU.add).then_inc(run_set, 1)
                    v.scalar_tensor_tensor(junk[:, 0, :], iota_row[:, 0:BINS], key, run[:, a_, :], ALU.is_equal, ALU.mult,
                                           accum_out=posf[:, u:u + 1]).then_inc(pos_got, 1)
                J = i * 2 + h
                dve.wait_ge(pos_got, i * 8 + HALF * h + HALF + 1)
                v.tensor_copy(posi[:, 0, :], posf[:, :]).then_inc(pos_step, 1)
                dve.wait_ge(pos_step, J * 3 + 1)
                v.tensor_single_scalar(posi[:, 1, :], posi[:, 0, :], 127, ALU.bitwise_and).then_inc(pos_step, 1)
                v.tensor_single_scalar(posi[:, 2, :], posi[:, 0, :], 7, ALU.logical_shift_right).then_inc(pos_step, 1)
                dve.wait_ge(pos_step, J * 3 + 3)
                if not first:
                    dve.wait_ge(s_sc[h], i * 64)
                v.scalar_tensor_tensor(idx_st[:, HALF * h:HALF * h + HALF], posi[:, 1, :], float(TCOL), posi[:, 2, :],
                                       ALU.mult, ALU.add).then_inc(pos_ready, 1)
                dve.wait_ge(pos_ready, J + 1)

            for h in range(2):
                positions(0, h, True)
            with dve.Fori(1, TPM // 8) as i:
                for h in range(2):
                    positions(i, h, False)
            dve.wait_ge(s_trow, 64)

            def tile_pass(p):
                dve.wait_ge(agg_zero, p)
                hots_and_adds(p, (0, 0), None, None, F)
                with dve.Fori(0, PAIRS - 1) as i:
                    b = blocks(p, i * 8)
                    hots_and_adds(p, (i, 1), (i, 0), b, F)
                    hots_and_adds(p, (i + 1, 0), (i, 1), b, F)
                b = blocks(p, (PAIRS - 1) * 8)
                hots_and_adds(p, (PAIRS - 1, 1), (PAIRS - 1, 0), b, F)
                hots_and_adds(p, None, (PAIRS - 1, 1), b, F)
                dve.wait_ge(agg_added, TILES * (p + 1) + 8)

            dve.wait_ge(s_ms, 16)
            tile_pass(1)
            dve.wait_ge(idx_staged, 2 * STAGES)
            dve.engine_nop().then_inc(pass_done, 1)
            step(v.tensor_tensor(Xa, Xa, Af, ALU.add))
            layernorm(Xa, TX)
            root()
            step(v.reciprocal(dinv[:, :], stat[:, 2, :]))
            root()
            step(v.reciprocal(vec[:, 6:7], vec[:, 6:7]))
            step(v.tensor_tensor(vec[:, 6:7], vec[:, 6:7], vec[:, 2:3], ALU.mult))
            step(v.tensor_tensor(vec[:, 7:8], vec[:, 6:7], vec[:, 4:5], ALU.mult))
            step(v.tensor_tensor(vec[:, 7:8], vec[:, 3:4], vec[:, 7:8], ALU.subtract))
            step(v.tensor_tensor(TX, Xa, wide(dinv[:, :]), ALU.mult))
            dve.engine_nop().then_inc(x_ready, 1)
            tile_pass(2)
            step(v.tensor_tensor(Af, Af, TX, ALU.add))
            step(v.tensor_tensor(Af, Af, wide(dinv[:, :]), ALU.mult))
            dve.engine_nop().then_inc(pass_done, 1)
            with dve.Fori(0, CHUNKS) as c:
                dve.wait_ge(z2_ev, c + 2)
                dve.wait_ge(bn_ready, c + 1)
                v.scalar_tensor_tensor(XT[0:F, :], GT, 0.05, GT, ALU.mult, ALU.max).then_inc(lk_done, 1)
                dve.wait_ge(lk_done, c + 2)
                dve.wait_ge(p_up, c + CHUNKS + 1)
                v.tensor_scalar(YT, XT[0:F, :], vec[:, 6:7], vec[:, 7:8], ALU.mult, ALU.add).then_inc(bn_ready, 1)
                dve.wait_ge(p_up, c + CHUNKS + 2)
                v.tensor_tensor(TX[:, ds(c * CH, CH), :], PS[6][:, 0:CH * F].rearrange("p (k f) -> p k f", k=CH),
                                dinv[:, ds(c * CH, CH)].unsqueeze(2).to_broadcast([P, CH, F]), ALU.mult).then_inc(h_done, 1)
            dve.wait_ge(h_done, 2 * CHUNKS + 1)
            dve.engine_nop().then_inc(x_ready, 1)
            tile_pass(3)
            step(v.tensor_tensor(Af, Af, TX, ALU.add))
            step(v.tensor_tensor(Af, Af, wide(dinv[:, :]), ALU.mult))
            step(v.tensor_tensor(Af, Af, per_feature(b2r[:, :]), ALU.add))
            dve.engine_nop().then_inc(pass_done, 1)
            step(v.tensor_tensor(Xa, Xa, Af, ALU.add))
            layernorm(Xa, TX)
            dve.engine_nop().then_inc(x_ready, 1)
            tile_pass(4)
            v.memset(Zf[F:F + 1, 512:1024], 1.0).then_inc(ones_row, 1)
            dve.engine_nop().then_inc(pass_done, 1)
            with dve.Fori(0, CHUNKS) as c:
                dve.wait_ge(p_tr, c + 2 * CHUNKS + 2)
                dve.wait_ge(p_up, c + 2 * CHUNKS + 1)
                v.tensor_copy(XT[0:F, :], PS[3][0:F, :]).then_inc(x_ev, 1)
                dve.wait_ge(p_up, c + 2 * CHUNKS + 2)
                v.tensor_copy(AGG[:, ds(c * CH, CH), 0:F], PS[6][:, 0:CH * F].rearrange("p (k f) -> p k f", k=CH)).then_inc(h_done, 1)
            dve.wait_ge(h_done, 3 * CHUNKS + 1)
            step(v.tensor_tensor(Xa, Xa, Af, ALU.add))
            layernorm(Xa, TX)
            dve.engine_nop().then_inc(x_ready, 1)


NAMES = {
    "mW1": "L0_gnn_mW1", "mb1": "L0_gnn_mb1", "mW2": "L0_gnn_mW2", "mb2": "L0_gnn_mb2",
    "gW1": "L0_gnn_gW1", "gb1": "L0_gnn_gb1", "gW2": "L0_gnn_gW2", "gb2": "L0_gnn_gb2",
    "uW1": "L0_gnn_uW1", "ub1": "L0_gnn_ub1", "uW2": "L0_gnn_uW2", "ub2": "L0_gnn_ub2",
    "ln_g": "L0_gnn_ln_g", "ln_b": "L0_gnn_ln_b", "W1": "L2_gnn_W1", "b1": "L2_gnn_b1",
    "W2": "L2_gnn_W2", "b2": "L2_gnn_b2", "bn_gamma": "L2_gnn_bn_gamma", "bn_beta": "L2_gnn_bn_beta",
    "bn_mean": "L2_gnn_bn_mean", "bn_var": "L2_gnn_bn_var", "mlp_b": "L3_gnn_mlp_b",
}


def kernel(**inputs):
    import numpy as np
    import concourse.bacc as bacc
    from concourse.bass_utils import run_bass_kernel_spmd

    def padded(v, fill):
        v = np.asarray(v)
        return np.concatenate([v, np.full((EPAD - E,), fill, v.dtype)])

    x = np.asarray(inputs["x"])
    xT = np.zeros((F, NPAD), x.dtype)
    xT[:, :N] = x.T
    ea = np.asarray(inputs["edge_attr_32"])
    eaT = np.zeros((EF, EPAD), ea.dtype)
    eaT[:, :E] = ea.T
    host = {
        "x": x, "xT": xT, "eaT": eaT,
        "src": padded(inputs["src"], NREAL * P), "dst": padded(inputs["dst"], NREAL * P),
        "w": padded(inputs["edge_weight"], 0), "mlp_wT": np.asarray(inputs["L3_gnn_mlp_w"]).T,
    }
    for short, name in NAMES.items():
        host[short] = np.asarray(inputs[name])
    nc = bacc.Bacc("TRN2", target_bir_lowering=False, num_devices=1)
    arrays, aps = {}, {}
    for name, v in host.items():
        v = np.ascontiguousarray(v)
        arrays[f"in_{name}"] = v
        aps[name] = nc.dram_tensor(f"in_{name}", v.shape, mybir.dt.from_np(v.dtype), kind="ExternalInput").ap()
    out = nc.dram_tensor("out", (N, F), mybir.dt.float32, kind="ExternalOutput").ap()
    build(nc, aps, out)
    r = run_bass_kernel_spmd(nc, [arrays], core_ids=[0])
    return r.results[0]["out"]
```

```python
import concourse.bass as bass
from concourse import mybir
from contextlib import ExitStack

N = 12500
F = 96
EF = 32
E = 200000
P = 128
EPS = 1e-5

NB = 100
NREAL = -(-N // P)
NPAD = NB * P
BINS = NREAL + 1
COPIES = 8

TPM = 1568
EPAD = P * TPM
TILES = 1664
assert (E + 127 * NREAL) // P <= TILES and TILES % P == 0 and EPAD - E >= P and TPM % 8 == 0
TCH = TILES // P
TCOL = TILES + 8
HALF = 4
HALVES = TILES // HALF
PAIRS = HALVES // 2
STAGES = HALVES + 2
MW = 98
CH = 4
CHUNKS = NB // CH


def build(nc, a, out):
    f32, i32, bf16 = mybir.dt.float32, mybir.dt.int32, mybir.dt.bfloat16
    ALU = mybir.AluOpType
    ACT = mybir.ActivationFunctionType
    AX = mybir.AxisListType
    DVE = mybir.EngineType.DVE
    SPE = mybir.EngineType.SP
    ds = bass.ds
    ctx = ExitStack()
    with ctx:
        def sb(name, shape, dt=f32):
            return ctx.enter_context(nc.sbuf_tensor(name, shape, dt))

        def sem(name):
            return ctx.enter_context(nc.semaphore(name))

        table0 = nc.dram_tensor("table0", (NPAD, 2 * F), f32).ap()
        table = {i: nc.dram_tensor(f"table{i}", (NPAD, F), f32).ap() for i in (2, 3, 4)}
        copy = [nc.dram_tensor(f"copy{i}", (NPAD + P, F), f32).ap() for i in range(COPIES)]
        tile_dram = nc.dram_tensor("tile_dram", (2 * TCH, P), i32).ap()

        X = sb("X", [P, NB, F])
        AGG = sb("AGG", [P, NB, MW])
        BIG = sb("BIG", [P, NB * F])
        MD = sb("MD", [P, 3, TCOL])
        tile_row = sb("tile_row", [1, 2 * TILES], i32)
        G = sb("G", [P, 8, 2 * F])
        Z = sb("Z", [P, 8, 2 * F])
        H = sb("H", [P, 8, 2 * F + 1])
        M = sb("M", [P, 8, MW])
        S = sb("S", [P, 8, P])
        CT = sb("CT", [P, 8, P])
        EA = CT[0:EF, :, :]
        zeros = sb("zeros", [P, 960])
        prod = sb("prod", [P, HALF, F])
        idx_st = sb("idx_st", [P, 8], i32)
        glin = sb("glin", [P, 8])
        gth = sb("gth", [P, 8])
        gate = sb("gate", [P, 8])
        iota_row = sb("iota_row", [P, P])
        iota_i = sb("iota_i", [P, P], i32)
        tile_id = sb("tile_id", [P, TCH])
        tile_id_i = sb("tile_id_i", [P, TCH], i32)
        part_i = sb("part_i", [P, P], i32)
        ident = sb("ident", [P, P])
        earlier = sb("earlier", [P, P])
        ones = sb("ones", [P, P])
        cnt = sb("cnt", [P, BINS])
        row_f = sb("row_f", [P, 6, BINS])
        row_i = sb("row_i", [P, 2, BINS], i32)
        junk = sb("junk", [P, 2, BINS])
        tcol = sb("tcol", [P, 4, TCH])
        repeats = sb("repeats", [P, 8])
        first = sb("first", [P, 8])
        spare = sb("spare", [P, 1])
        spare_i = sb("spare_i", [P, 1], i32)
        from_spare = sb("from_spare", [P, 8])
        tcol_i = sb("tcol_i", [P, TCH], i32)
        tp_i = sb("tp_i", [2 * TCH, P], i32)
        stat = sb("stat", [P, 3, NB])
        deg = sb("deg", [P, NB])
        dinv = sb("dinv", [P, NB])
        W0 = sb("W0", [F + 1, 2 * F])
        WE = sb("WE", [EF, 2 * F])
        gw2 = sb("gw2", [P, F])
        gb2 = sb("gb2", [P, 1])
        hgb2 = sb("hgb2", [P, 1])
        W2a = sb("W2a", [F + 1, F])
        U1x = sb("U1x", [F, F])
        U1g = sb("U1g", [F, F])
        U2 = sb("U2", [F + 1, F])
        lng = sb("lng", [P, F])
        lnb = sb("lnb", [P, F])
        C1 = sb("C1", [F, F])
        C2 = sb("C2", [F, F])
        b2r = sb("b2r", [P, F])
        L3x = sb("L3x", [F + 1, F])
        L3g = sb("L3g", [F, F])
        vec = sb("vec", [F, 8])
        eps = sb("eps", [P, 1])
        Gf = G[:, :, :].rearrange("p a b -> p (a b)")
        Zf = Z[:, :, :].rearrange("p a b -> p (a b)")
        Hf = H[:, :, :].rearrange("p a b -> p (a b)")
        AS = Gf[:, 0:CH * 97].rearrange("p (k f) -> p k f", k=CH)
        XS = Gf[:, 512:512 + CH * F].rearrange("p (k f) -> p k f", k=CH)
        AT = Zf[0:F + 1, 0:CH * P]
        XT = Zf[0:F + 1, 512:1024]
        GT = Zf[0:F, 1024:1536]
        UT = Hf[0:F + 1, 0:512]
        YT = Hf[0:F, 512:1024]
        DIAG = Zf[:, 0:8 * P].rearrange("p (t e) -> p t e", e=P)
        SAME = Hf[:, 0:8 * P].rearrange("p (t e) -> p t e", e=P)
        MSG = Gf[:, 0:8 * F].rearrange("p (t f) -> p t f", f=F)
        pm_dst = BIG[:, 0:TPM].bitcast(i32)
        hi_i = BIG[:, TPM:2 * TPM].bitcast(i32)
        hi_f = BIG[:, 2 * TPM:2 * TPM + TPM // 2].bitcast(bf16)
        hjunk = BIG[:, 3 * TPM:3 * TPM + TPM // 2].bitcast(bf16)
        ROWS = BIG[:, 0:3 * TCH * P].rearrange("p (k c e) -> p k c e", k=3, e=P)
        ROWI = BIG[:, 3 * TCH * P:5 * TCH * P].bitcast(i32).rearrange("p (k c e) -> p k c e", k=2, e=P)
        TX = BIG[:, :].rearrange("p (b f) -> p b f", f=F)
        Af = AGG[:, :, 0:F]
        T0X = [Zf[0:F + 1, 0:256], Zf[0:F + 1, 256:512]]
        T0S = [Gf[:, 0:384], Gf[:, 384:768]]

        LOADS = 29

        PS = [ctx.enter_context(nc.psum_tensor(f"bank{i}", [P, 512], f32)) for i in range(8)]
        seg_bank = [PS[0], PS[1]]
        z_bank = [[PS[2], PS[3]], [PS[4], PS[5]]]

        s_load = sem("s_load")
        s_pm = sem("s_pm")
        const_ready = sem("const_ready")
        dve_step = sem("dve_step")
        act_step = sem("act_step")
        cnt_ready = sem("cnt_ready")
        tot_ready = sem("tot_ready")
        tiles_known = sem("tiles_known")
        tcol_t = sem("tcol_t")
        trow_out = sem("trow_out")
        s_trow = sem("s_trow")
        s_rows = sem("s_rows")
        rows_f = sem("rows_f")
        rows_t = sem("rows_t")
        md_ready = sem("md_ready")
        s_xt = [sem("s_xt0"), sem("s_xt1")]
        t0_mm = sem("t0_mm")
        t0_ev = sem("t0_ev")
        s_t0 = [sem("s_t00"), sem("s_t01")]
        idx_staged = sem("idx_staged")
        s_g = [[sem(f"s_g{p}_{h}") for h in range(2)] for p in range(5)]
        s_ea = [sem("s_ea0"), sem("s_ea1")]
        z_mm = sem("z_mm")
        z_added = sem("z_added")
        h_ready = sem("h_ready")
        prod_ready = sem("prod_ready")
        lin_ready = sem("lin_ready")
        th_ready = sem("th_ready")
        gate_ready = sem("gate_ready")
        m_ready = sem("m_ready")
        s_ready = sem("s_ready")
        seg_done = sem("seg_done")
        agg_added = sem("agg_added")
        pass_done = sem("pass_done")
        p_staged = sem("p_staged")
        p_tr = sem("p_tr")
        a_ev = sem("a_ev")
        x_ev = sem("x_ev")
        p_gt = sem("p_gt")
        g_ev = sem("g_ev")
        p_u = sem("p_u")
        u_ev = sem("u_ev")
        p_up = sem("p_up")
        h_done = sem("h_done")
        act_sqrt = sem("act_sqrt")
        var_ready = sem("var_ready")
        s_zero = sem("s_zero")
        diag_ready = sem("diag_ready")
        bc_done = sem("bc_done")
        same_ready = sem("same_ready")
        ct_done = sem("ct_done")
        ct_ev = sem("ct_ev")
        msg_done = sem("msg_done")
        msg_ev = sem("msg_ev")
        rep_done = sem("rep_done")
        first_done = sem("first_done")
        sc_idx = sem("sc_idx")
        s_sc = [sem(f"s_sc{u}") for u in range(COPIES)]
        s_back = [sem("s_back0"), sem("s_back1")]
        copy_added = sem("copy_added")
        x_ready = sem("x_ready")
        agg_zero = sem("agg_zero")
        s_table = sem("s_table")
        s_out = sem("s_out")
        ones_row = sem("ones_row")
        hist_step = sem("hist_step")
        z2_ev = sem("z2_ev")
        lk_done = sem("lk_done")
        bn_ready = sem("bn_ready")
        block = ctx.enter_context(nc.Block())

        def chain(eng, semaphore):
            count = [0]

            def step(ins):
                count[0] += 1
                ins.then_inc(semaphore, 1)
                eng.wait_ge(semaphore, count[0])
            return step

        def table_view(ap):
            return ap.rearrange("(p b) f -> p b f", p=P)

        def meta(k, t0, n):
            return MD[:, k, ds(t0, n)]

        def turn(p):
            return p if p == 0 else p - 1

        WEIGHTED = (False, True, False, False, True)

        @block.sync
        def _(sp):
            sp.dma_start(pm_dst, a["dst"].rearrange("(p t) -> p t", p=P)).then_inc(s_pm, 16)
            loads = [
                (X[:, :, :], a["x"]),
                (W0[0:F, 0:F], a["gW1"][0:F, :]), (W0[0:F, F:2 * F], a["mW1"][0:F, :]),
                (W0[F:F + 1, 0:F], a["gb1"].unsqueeze(0)), (W0[F:F + 1, F:2 * F], a["mb1"].unsqueeze(0)),
                (WE[:, 0:F], a["gW1"][F:F + EF, :]), (WE[:, F:2 * F], a["mW1"][F:F + EF, :]),
                (gw2[:, :], a["gW2"].rearrange("f a -> (a f)").partition_broadcast(P)),
                (gb2[:, :], a["gb2"].partition_broadcast(P)),
                (W2a[0:F, :], a["mW2"]), (W2a[F:F + 1, :], a["mb2"].unsqueeze(0)),
                (U1x[:, :], a["uW1"][0:F, :]), (U1g[:, :], a["uW1"][F:2 * F, :]),
                (U2[0:F, :], a["uW2"]), (U2[F:F + 1, :], a["ub2"].unsqueeze(0)),
                (lng[:, :], a["ln_g"].partition_broadcast(P)), (lnb[:, :], a["ln_b"].partition_broadcast(P)),
                (C1[:, :], a["W1"]), (C2[:, :], a["W2"]), (b2r[:, :], a["b2"].partition_broadcast(P)),
                (L3x[0:F, :], a["mlp_wT"][0:F, :]), (L3x[F:F + 1, :], a["mlp_b"].unsqueeze(0)),
                (L3g[:, :], a["mlp_wT"][F:2 * F, :]),
            ] + [(vec[:, i:i + 1], a[n].unsqueeze(1)) for i, n in enumerate(("ub1", "b1", "bn_gamma", "bn_beta", "bn_mean", "bn_var"))]
            for o, i in loads:
                sp.dma_start(o, i).then_inc(s_load, 16)
            assert len(loads) == LOADS
            with sp.Fori(0, NB // 4) as i:
                for h in range(2):
                    sp.wait_ge(t0_mm, i * 2 + h + 1)
                    sp.nop(nofuse=True)
                    sp.dma_start(T0X[h][0:F, :], a["xT"][:, ds(i * 512 + h * 256, 256)]).then_inc(s_xt[h], 16)
            sp.wait_ge(trow_out, 1)
            sp.dma_start(tile_dram, tp_i[:, :]).then_inc(s_trow, 16)
            sp.wait_ge(s_trow, 16)
            sp.dma_start(tile_row[0:1, :], tile_dram.rearrange("(o c) p -> o (c p)", o=1)).then_inc(s_trow, 16)
            sp.wait_ge(s_trow, 32)
            with sp.Fori(0, PAIRS) as i:
                _, first = nc.values_load_multi_w_load_instructions(
                    tile_row[0:1, ds(i * 8 + TILES, 8)], engines=[SPE], min_val=0, max_val=EPAD - P,
                    skip_runtime_bounds_check_because="DVE clamps the first edge to EPAD - 128")
                for h in range(2):
                    sp.wait_ge(z_mm, i * 2 + h + 1)
                    sp.nop(nofuse=True)
                    for u in range(HALF):
                        sp.dma_start(EA[:, HALF * h + u, :], a["eaT"][:, ds(first[HALF * h + u], P)]).then_inc(s_ea[h], 16)
            for k in range(COPIES):
                sp.wait_ge(s_sc[k], 16 * PAIRS)
            for k in range(COPIES):
                if k >= 2:
                    sp.wait_ge(copy_added, k - 1)
                sp.dma_start((Af, TX)[k % 2], table_view(copy[k][0:NPAD, :])).then_inc(s_back[k % 2], 16)
            for p, on_chip in ((2, TX), (3, TX), (4, X[:, :, :])):
                sp.wait_ge(x_ready, p)
                sp.dma_start(table_view(table[p]), on_chip).then_inc(s_table, 16)
            sp.wait_ge(x_ready, 5)
            sp.dma_start(out, X[:, :, :]).then_inc(s_out, 16)
            sp.wait_ge(s_out, 16)

        @block.gpsimd
        def _(pool):
            pool.iota(iota_i[:, :], pattern=[[1, P]], base=0, channel_multiplier=0).then_inc(const_ready, 1)
            pool.iota(part_i[:, :], pattern=[[0, P]], base=0, channel_multiplier=1).then_inc(const_ready, 1)
            pool.iota(tile_id_i[:, :], pattern=[[P, TCH]], base=0, channel_multiplier=1).then_inc(const_ready, 1)
            pool.memset(ones[:, :], 1.0).then_inc(const_ready, 1)
            pool.memset(H[:, :, 2 * F:2 * F + 1], 1.0).then_inc(const_ready, 1)
            pool.memset(M[:, :, MW - 1:MW], 1.0).then_inc(const_ready, 1)
            pool.memset(zeros[:, :], 0.0).then_inc(const_ready, 1)
            pool.memset(AGG[:, :, :], 0.0).then_inc(const_ready, 1)
            pool.iota(spare_i[:, :], pattern=[[0, 1]], base=NPAD, channel_multiplier=1).then_inc(const_ready, 1)
            pool.memset(MD[:, :, TILES:TCOL], 0.0).then_inc(const_ready, 1)
            pool.memset(eps[:, :], EPS).then_inc(const_ready, 1)
            pool.wait_ge(tiles_known, 1)
            pool.nop(nofuse=True)
            for c in range(TCH):
                for k, n in enumerate(("src", "dst", "w")):
                    o = ROWS[:, k, c, :] if k == 2 else ROWS[:, k, c, :].bitcast(i32)
                    pool.indirect_dma_start(out=o, out_offset=None, in_=a[n].rearrange("(n a) -> n a", a=1),
                                            in_offset=bass.IndirectOffsetOnAxis(ap=tcol_i[:, c:c + 1], axis=0)).then_inc(s_rows, 16)

            def gathers(p, src_table, width):
                with pool.Fori(0, PAIRS) as i:
                    for h in range(2):
                        pool.wait_ge(idx_staged, i * 2 + (STAGES * turn(p) + h + 1))
                        if p == 0:
                            pool.wait_ge(z_added, i * 2 + h + 1)
                        else:
                            pool.wait_ge(seg_done, i * 2 + (HALVES * turn(p) + h + 1))
                        pool.nop(nofuse=True)
                        for u in range(HALF * h, HALF * h + HALF):
                            pool.indirect_dma_start(
                                out=G[:, u, 0:width], out_offset=None, in_=src_table,
                                in_offset=bass.IndirectOffsetOnAxis(ap=idx_st[:, u:u + 1], axis=0)).then_inc(s_g[p][h], 16)

            def stage(c, first, x_too, width):
                pool.wait_ge(p_tr, c + first + 1)
                pool.tensor_copy(AS[:, :, 0:width], AGG[:, ds(c * CH, CH), 0:width]).then_inc(p_staged, 1)
                if x_too:
                    pool.tensor_copy(XS[:, :, :], X[:, ds(c * CH, CH), :]).then_inc(p_staged, 1)

            for h in range(2):
                pool.wait_ge(s_t0[h], 16 * (NB // 4))
            pool.wait_ge(t0_mm, NB // 2 + 2)
            gathers(0, table0, 2 * F)
            pool.wait_ge(pass_done, 1)
            with pool.Fori(0, CHUNKS) as c:
                stage(c, 0, True, 97)
            pool.wait_ge(s_zero, 16 * 2 * COPIES)
            with pool.Fori(0, PAIRS) as i:
                for h in range(2):
                    pool.wait_ge(sc_idx, i * 2 + h + 1)
                    pool.wait_ge(msg_ev, i * 2 + h + 3)
                    pool.nop(nofuse=True)
                    for u in range(HALF * h, HALF * h + HALF):
                        pool.indirect_dma_start(
                            out=copy[u], out_offset=bass.IndirectOffsetOnAxis(ap=idx_st[:, u:u + 1], axis=0),
                            in_=MSG[:, u, :], in_offset=None, compute_op=ALU.add).then_inc(s_sc[u], 16)
            for p in (2, 3, 4):
                pool.wait_ge(x_ready, p)
                pool.memset(AGG[:, :, :], 0.0).then_inc(agg_zero, 1)
                pool.wait_ge(s_table, 16 * (p - 1))
                gathers(p, table[p], F)
                pool.wait_ge(pass_done, p)
                if p == 2:
                    with pool.Fori(0, CHUNKS) as c:
                        stage(c, CHUNKS, False, F)
                if p == 4:
                    with pool.Fori(0, CHUNKS) as c:
                        stage(c, 2 * CHUNKS, True, F)

        @block.tensor
        def _(pe):
            mm = nc.tensor.matmul
            for s in (t0_mm, bc_done, ct_done, msg_done):
                pe.sem_inc(s, 2)
            pe.sem_inc(seg_done, 2)
            pe.sem_inc(z_mm, 2)
            for s in (p_tr, p_gt, p_u, p_up):
                pe.sem_inc(s, 1)
            pe.wait_ge(s_load, 16 * LOADS)
            pe.wait_ge(ones_row, 1)
            with pe.Fori(0, NB // 4) as i:
                for h in range(2):
                    pe.wait_ge(s_xt[h], i * 16 + 16)
                    pe.wait_ge(t0_ev, i * 2 + h + 1)
                    for k in range(2):
                        last = mm(z_bank[0][h][:, k * 192:(k + 1) * 192], T0X[h][:, k * P:(k + 1) * P], W0[:, :], start=True, stop=True)
                    last.then_inc(t0_mm, 1)

            pe.wait_ge(cnt_ready, 1)
            mm(PS[6][:, 0:BINS], ones[:, :], cnt[:, :], start=True, stop=True).then_inc(tot_ready, 1)
            pe.wait_ge(tiles_known, 1)
            nc.tensor.transpose(PS[7][0:2 * TCH, 0:P], tcol[:, 0:2, :].rearrange("p a c -> p (a c)"), ident[:, :]).then_inc(tcol_t, 1)
            for c in range(TCH):
                pe.wait_ge(rows_f, 1)
                if c >= 2:
                    pe.wait_ge(md_ready, c - 1)
                for k in range(3):
                    last = nc.tensor.transpose(seg_bank[c % 2][:, k * P:(k + 1) * P], ROWS[:, k, c, :], ident[:, :])
                last.then_inc(rows_t, 1)

            def z_half(i, h):
                pe.wait_ge(s_ea[h], i * 64 + 64)
                pe.wait_ge(z_added, i * 2 + h + 1)
                for u in range(HALF):
                    last = mm(z_bank[h][u // 2][:, (u % 2) * 192:(u % 2) * 192 + 192], EA[:, HALF * h + u, :], WE[:, :], start=True, stop=True)
                last.then_inc(z_mm, 1)

            def seg_half(p, i, h, width):
                if p == 0:
                    pe.wait_ge(m_ready, i * 2 + h + 1)
                else:
                    pe.wait_ge(s_g[p][h], i * 64 + 64)
                pe.wait_ge(s_ready, i * 2 + (HALVES * turn(p) + h + 1))
                pe.wait_ge(agg_added, i * 8 + (TILES * turn(p) + 4 * h + 4))
                for u in range(HALF):
                    rhs = M[:, HALF * h + u, :] if p == 0 else G[:, HALF * h + u, 0:F]
                    last = mm(seg_bank[h][:, u * P:u * P + width], S[:, HALF * h + u, :], rhs, start=True, stop=True)
                last.then_inc(seg_done, 1)

            pe.wait_ge(md_ready, TCH)
            pe.wait_ge(t0_ev, NB // 2 + 2)
            z_half(0, 0)
            z_half(0, 1)
            with pe.Fori(0, PAIRS - 1) as i:
                z_half(i + 1, 0)
                seg_half(0, i, 0, MW)
                z_half(i + 1, 1)
                seg_half(0, i, 1, MW)
            seg_half(0, PAIRS - 1, 0, MW)
            seg_half(0, PAIRS - 1, 1, MW)

            def transposes(c, first, staged0, staged, width, x_too):
                pe.wait_ge(p_staged, c * staged + (staged0 + staged))
                pe.wait_ge(a_ev, c + first + 1)
                pe.wait_ge(x_ev, c + min(first, CHUNKS) + 1) if x_too else None
                for k in range(CH):
                    last = nc.tensor.transpose(PS[2][0:width, k * P:(k + 1) * P], AS[:, k, 0:width], ident[:, :])
                if x_too:
                    for k in range(CH):
                        last = nc.tensor.transpose(PS[3][0:F, k * P:(k + 1) * P], XS[:, k, :], ident[:, :])
                last.then_inc(p_tr, 1)

            pe.wait_ge(ones_row, 2)
            with pe.Fori(0, CHUNKS) as c:
                transposes(c, 0, 0, 2, 97, True)
                pe.wait_ge(a_ev, c + 2)
                pe.wait_ge(g_ev, c + 1)
                mm(PS[4][0:F, :], W2a[:, :], AT, start=True, stop=True).then_inc(p_gt, 1)
                pe.wait_ge(g_ev, c + 2)
                pe.wait_ge(x_ev, c + 2)
                pe.wait_ge(u_ev, c + 1)
                mm(PS[5][0:F, :], U1x[:, :], XT[0:F, :], start=True, stop=False)
                mm(PS[5][0:F, :], U1g[:, :], GT, start=False, stop=True).then_inc(p_u, 1)
                pe.wait_ge(u_ev, c + 2)
                pe.wait_ge(h_done, c + 1)
                for k in range(CH):
                    last = mm(PS[6][:, k * F:(k + 1) * F], UT[:, k * P:(k + 1) * P], U2[:, :], start=True, stop=True)
                last.then_inc(p_up, 1)
            def spread(i, h):
                pe.wait_ge(diag_ready, i * 2 + h + 1)
                pe.wait_ge(same_ready, i * 2 + h + 1)
                for u in range(HALF * h, HALF * h + HALF):
                    last = mm(PS[h][:, (u % HALF) * P:(u % HALF + 1) * P], ones[:, :], DIAG[:, u, :], start=True, stop=True)
                last.then_inc(bc_done, 1)

            def messages(i, h, b):
                pe.wait_ge(same_ready, i * 2 + h + 3)
                pe.wait_ge(ct_ev, i * 2 + h + 1)
                for u in range(HALF * h, HALF * h + HALF):
                    last = mm(PS[2 + h][:, (u % HALF) * P:(u % HALF + 1) * P], S[:, u, :], SAME[:, u, :], start=True, stop=True)
                last.then_inc(ct_done, 1)
                pe.wait_ge(ct_ev, i * 2 + h + 3)
                pe.wait_ge(msg_ev, i * 2 + h + 1)
                for u in range(HALF * h, HALF * h + HALF):
                    last = mm(PS[4 + h][:, (u % HALF) * F:(u % HALF + 1) * F], CT[:, u, :],
                              X[:, ds(b[u], 1), :].rearrange("p b f -> p (b f)"), start=True, stop=True)
                last.then_inc(msg_done, 1)

            def tile_blocks(i):
                _, b = nc.values_load_multi_w_load_instructions(
                    tile_row[0:1, ds(i * 8, 8)], engines=[mybir.EngineType.PE], min_val=0, max_val=NREAL,
                    skip_runtime_bounds_check_because="the block of a tile is clamped to NREAL when it is computed")
                return b

            pe.wait_ge(x_ready, 1)
            spread(0, 0)
            with pe.Fori(0, PAIRS - 1) as i:
                b = tile_blocks(i)
                spread(i, 1)
                messages(i, 0, b)
                spread(i + 1, 0)
                messages(i, 1, b)
            b = tile_blocks(PAIRS - 1)
            spread(PAIRS - 1, 1)
            messages(PAIRS - 1, 0, b)
            messages(PAIRS - 1, 1, b)

            def agg_pass(p):
                with pe.Fori(0, PAIRS) as i:
                    for h in range(2):
                        seg_half(p, i, h, F)

            agg_pass(2)
            with pe.Fori(0, CHUNKS) as c:
                transposes(c, CHUNKS, 2 * CHUNKS, 1, F, False)
                pe.wait_ge(a_ev, c + CHUNKS + 2)
                pe.wait_ge(z2_ev, c + 1)
                mm(PS[4][0:F, :], C1[:, :], AT[0:F, :], start=True, stop=True).then_inc(p_gt, 1)
                pe.wait_ge(bn_ready, c + 2)
                pe.wait_ge(h_done, c + CHUNKS + 1)
                for k in range(CH):
                    last = mm(PS[6][:, k * F:(k + 1) * F], YT[:, k * P:(k + 1) * P], C2[:, :], start=True, stop=True)
                last.then_inc(p_up, 1)
            agg_pass(3)
            agg_pass(4)
            pe.wait_ge(ones_row, 3)
            with pe.Fori(0, CHUNKS) as c:
                transposes(c, 2 * CHUNKS, 3 * CHUNKS, 2, F, True)
                pe.wait_ge(a_ev, c + 2 * CHUNKS + 2)
                pe.wait_ge(x_ev, c + CHUNKS + 2)
                pe.wait_ge(h_done, c + 2 * CHUNKS + 1)
                for k in range(CH):
                    mm(PS[6][:, k * F:(k + 1) * F], XT[:, k * P:(k + 1) * P], L3x[:, :], start=True, stop=False)
                    last = mm(PS[6][:, k * F:(k + 1) * F], AT[0:F, k * P:(k + 1) * P], L3g[:, :], start=False, stop=True)
                last.then_inc(p_up, 1)

        @block.scalar
        def _(act):
            step = chain(act, act_step)
            act_fn = nc.scalar.activation
            act.sem_inc(t0_ev, 2)
            act.sem_inc(a_ev, 1)
            act.sem_inc(ct_ev, 2)
            act.sem_inc(msg_ev, 2)
            act.sem_inc(u_ev, 1)
            act.sem_inc(z2_ev, 1)

            def t0_half(i, h, again):
                act.wait_ge(t0_mm, i * 2 + h + 3)
                if again:
                    act.wait_ge(s_t0[h], i * 16)
                act_fn(T0S[h], z_bank[0][h][:, 0:384], ACT.Copy).then_inc(t0_ev, 1)
                act.wait_ge(t0_ev, i * 2 + h + 3)
                act.dma_start(table_view(table0)[:, ds(i * 4 + h * 2, 2), :].rearrange("p b f -> p (b f)"), T0S[h]).then_inc(s_t0[h], 16)

            for h in range(2):
                t0_half(0, h, False)
            with act.Fori(1, NB // 4) as i:
                for h in range(2):
                    t0_half(i, h, True)
            act.wait_ge(const_ready, 11)
            for c in copy:
                act.dma_start(c[0:NPAD, :].rearrange("(p a b) f -> p a (b f)", p=P, a=10),
                              zeros[:, :].unsqueeze(1).to_broadcast([P, 10, 960])).then_inc(s_zero, 16)
                act.dma_start(c[NPAD:NPAD + P, :], zeros[:, 0:F]).then_inc(s_zero, 16)
            step(act_fn(hgb2[:, :], gb2[:, :], ACT.Copy, scale=0.5))

            def stage(p, i, h):
                act.wait_ge(idx_staged, i * 2 + (STAGES * turn(p) + h)) if not (p == 0 and isinstance(i, int) and i == 0) else None
                act_fn(idx_st[:, HALF * h:HALF * h + HALF], meta(0, i * 8 + HALF * h, HALF), ACT.Copy).then_inc(idx_staged, 1)

            def gelu(i, h):
                act.wait_ge(z_added, i * 2 + h + 3)
                act.wait_ge(m_ready, i * 2 + h - 1) if not isinstance(i, int) else None
                act_fn(H[:, HALF * h:HALF * h + HALF, 0:2 * F], Z[:, HALF * h:HALF * h + HALF, :], ACT.Gelu).then_inc(h_ready, 1)

            def tanh(i, h):
                act.wait_ge(lin_ready, i * 2 + h + 1)
                act_fn(gth[:, HALF * h:HALF * h + HALF], glin[:, HALF * h:HALF * h + HALF], ACT.Tanh, bias=hgb2[:, :], scale=0.5).then_inc(th_ready, 1)

            act.wait_ge(md_ready, TCH)
            stage(0, 0, 0)
            act.wait_ge(idx_staged, 1)
            act_fn(idx_st[:, HALF:2 * HALF], meta(0, HALF, HALF), ACT.Copy).then_inc(idx_staged, 1)
            gelu(0, 0)
            stage(0, 1, 0)
            gelu(0, 1)
            stage(0, 1, 1)
            tanh(0, 0)
            with act.Fori(1, PAIRS) as i:
                gelu(i, 0)
                stage(0, i + 1, 0)
                tanh(i - 1, 1)
                gelu(i, 1)
                stage(0, i + 1, 1)
                tanh(i, 0)
            tanh(PAIRS - 1, 1)

            with act.Fori(0, CHUNKS) as c:
                act.wait_ge(p_tr, c + 2)
                act.wait_ge(p_gt, c + 1)
                act_fn(AT, PS[2][0:F + 1, :], ACT.Copy).then_inc(a_ev, 1)
                act.wait_ge(p_u, c + 2)
                act.wait_ge(p_up, c + 1)
                act_fn(UT[0:F, :], PS[5][0:F, :], ACT.Gelu, bias=vec[:, 0:1]).then_inc(u_ev, 1)

            sqrts = [0]

            def sqrt(o, i, scale, bias):
                sqrts[0] += 1
                act.wait_ge(var_ready, sqrts[0])
                act_fn(o, i, ACT.Sqrt, bias=bias, scale=scale).then_inc(act_sqrt, 1)

            def ln_sqrt():
                sqrt(stat[:, 2, :], stat[:, 1, :], 1.0 / F, eps[:, :])

            ln_sqrt()
            ln_sqrt()

            def ct_copy(i, h):
                act.wait_ge(ct_done, i * 2 + h + 3)
                act.wait_ge(msg_done, i * 2 + h + 1)
                act_fn(CT[:, HALF * h:HALF * h + HALF, :], PS[2 + h][:, :].rearrange("p (t e) -> p t e", e=P), ACT.Copy).then_inc(ct_ev, 1)

            def msg_copy(i, h, again):
                act.wait_ge(msg_done, i * 2 + h + 3)
                if again:
                    for u in range(HALF * h, HALF * h + HALF):
                        act.wait_ge(s_sc[u], i * 16)
                act_fn(MSG[:, HALF * h:HALF * h + HALF, :], PS[4 + h][:, 0:HALF * F].rearrange("p (t f) -> p t f", f=F), ACT.Copy).then_inc(msg_ev, 1)

            act.wait_ge(x_ready, 1)
            for h in range(2):
                ct_copy(0, h)
                msg_copy(0, h, False)
            with act.Fori(1, PAIRS) as i:
                for h in range(2):
                    ct_copy(i, h)
                    msg_copy(i, h, True)

            def stagings(p):
                act.wait_ge(x_ready, p)
                for h in range(2):
                    act.wait_ge(idx_staged, STAGES * turn(p) + h)
                    act_fn(idx_st[:, HALF * h:HALF * h + HALF], meta(0, HALF * h, HALF), ACT.Copy).then_inc(idx_staged, 1)
                with act.Fori(0, PAIRS) as i:
                    for h in range(2):
                        act.wait_ge(s_g[p][h], i * 64 + 64)
                        stage(p, i + 1, h)

            ln_sqrt()
            sqrt(stat[:, 2, :], deg[:, :], 1.0, 0.0)
            sqrt(vec[:, 6:7], vec[:, 5:6], 1.0, eps[0:F, :])
            stagings(2)
            with act.Fori(0, CHUNKS) as c:
                act.wait_ge(p_tr, c + CHUNKS + 2)
                act.wait_ge(p_gt, c + CHUNKS + 1)
                act_fn(AT[0:F, :], PS[2][0:F, :], ACT.Copy).then_inc(a_ev, 1)
                act.wait_ge(p_gt, c + CHUNKS + 2)
                act.wait_ge(lk_done, c + 1)
                act_fn(GT, PS[4][0:F, :], ACT.Identity, bias=vec[:, 1:2]).then_inc(z2_ev, 1)
            stagings(3)
            ln_sqrt()
            stagings(4)
            with act.Fori(0, CHUNKS) as c:
                act.wait_ge(p_tr, c + 2 * CHUNKS + 2)
                act.wait_ge(p_up, c + 2 * CHUNKS + 1)
                act_fn(AT[0:F, :], PS[2][0:F, :], ACT.Copy).then_inc(a_ev, 1)
            ln_sqrt()

        @block.vector
        def _(dve):
            step = chain(dve, dve_step)
            v = nc.vector
            dve.sem_inc(z_added, 2)
            dve.sem_inc(same_ready, 2)
            dve.sem_inc(agg_added, 8)
            for s in (x_ev, g_ev, h_done, lk_done, bn_ready):
                dve.sem_inc(s, 1)
            v.memset(Zf[F:F + 1, 0:512], 1.0).then_inc(ones_row, 1)
            dve.wait_ge(const_ready, 11)
            step(v.tensor_copy(iota_row[:, :], iota_i[:, :]))
            step(v.tensor_copy(tile_id[:, :], tile_id_i[:, :]))
            step(v.tensor_tensor(ident[:, :], iota_i[:, :], part_i[:, :], ALU.is_equal))
            step(v.tensor_tensor(earlier[:, :], iota_i[:, :], part_i[:, :], ALU.is_lt))
            step(v.tensor_copy(spare[:, :], spare_i[:, :]))

            dve.wait_ge(s_pm, 16)
            step(v.tensor_single_scalar(hi_i, pm_dst, 7, ALU.logical_shift_right))
            step(v.tensor_copy(hi_f, hi_i))
            with dve.Fori(0, BINS) as b:
                v.tensor_scalar(hjunk, hi_f, iota_row[:, ds(b, 1)], None, ALU.is_equal, ALU.add,
                                accum_out=cnt[:, ds(b, 1)]).then_inc(hist_step, 1)
                dve.wait_ge(hist_step, b + 1)
            dve.engine_nop().then_inc(cnt_ready, 1)
            c, nt, ti, dg, one = (row_f[:, k, :] for k in range(5))
            step(v.memset(one, 1.0))
            dve.wait_ge(tot_ready, 1)
            step(v.tensor_copy(c, PS[6][:, 0:BINS]))
            step(v.memset(c[:, NREAL:BINS], 0.0))
            step(v.tensor_scalar(row_i[:, 0, :], c, 127.0, None, ALU.add))
            step(v.tensor_single_scalar(row_i[:, 1, :], row_i[:, 0, :], 7, ALU.logical_shift_right))
            step(v.tensor_copy(nt, row_i[:, 1, :]))
            step(v.tensor_tensor_scan(ti, one, nt, 0.0, ALU.mult, ALU.add))
            step(v.scalar_tensor_tensor(dg, nt, -128.0, c, ALU.mult, ALU.add))
            for k in range(TCH):
                v.tensor_scalar(junk[:, 0, :], ti, tile_id[:, k:k + 1], None, ALU.is_le, ALU.add,
                                accum_out=tcol[:, 0, k:k + 1])
                step(v.scalar_tensor_tensor(junk[:, 1, :], ti, tile_id[:, k:k + 1], dg, ALU.is_le, ALU.mult,
                                            accum_out=tcol[:, 1, k:k + 1]))
            step(v.tensor_scalar(tcol[:, 0, :], tcol[:, 0, :], float(NREAL), None, ALU.min))
            step(v.scalar_tensor_tensor(tcol[:, 1, :], tile_id[:, :], 128.0, tcol[:, 1, :], ALU.mult, ALU.add))
            step(v.tensor_scalar(tcol[:, 1, :], tcol[:, 1, :], float(EPAD - P), None, ALU.min))
            step(v.tensor_scalar(tcol[:, 2, :], tcol[:, 0, :], 128.0, None, ALU.mult))
            step(v.tensor_copy(tcol_i[:, :], tcol[:, 1, :]))
            dve.engine_nop().then_inc(tiles_known, 1)
            dve.wait_ge(tcol_t, 1)
            step(v.tensor_copy(tp_i[:, :], PS[7][0:2 * TCH, 0:P]))
            dve.engine_nop().then_inc(trow_out, 1)

            dve.wait_ge(s_rows, 16 * 3 * TCH)
            src_i = ROWS[:, 0, :, :].bitcast(i32)
            step(v.tensor_single_scalar(ROWI[:, 0, :, :], src_i, 127, ALU.bitwise_and))
            step(v.tensor_single_scalar(ROWI[:, 1, :, :], src_i, 7, ALU.logical_shift_right))
            step(v.scalar_tensor_tensor(ROWS[:, 0, :, :], ROWI[:, 0, :, :], float(NB), ROWI[:, 1, :, :], ALU.mult, ALU.add))
            step(v.tensor_copy(ROWI[:, 0, :, :], ROWS[:, 1, :, :].bitcast(i32)))
            v.tensor_tensor(ROWS[:, 1, :, :], ROWI[:, 0, :, :], tcol[:, 2, :].unsqueeze(2).to_broadcast([P, TCH, P]),
                            ALU.subtract).then_inc(rows_f, 1)
            for c in range(TCH):
                dve.wait_ge(rows_t, c + 1)
                v.tensor_copy(MD[:, :, c * P:(c + 1) * P], seg_bank[c % 2][:, 0:3 * P].rearrange("p (k e) -> p k e", k=3)).then_inc(md_ready, 1)
            dve.wait_ge(md_ready, TCH)
            dve.wait_ge(s_trow, 32)

            def blocks(col):
                _, b = nc.values_load_multi_w_load_instructions(
                    tile_row[0:1, ds(col, 8)], engines=[DVE], min_val=0, max_val=NREAL,
                    skip_runtime_bounds_check_because="the block of a tile is clamped to NREAL when it is computed")
                return b

            def one_hot(p, i, h, u):
                slot = HALF * h + u
                lo = meta(1, i * 8 + slot, 1)
                if WEIGHTED[p]:
                    ins = v.tensor_scalar(S[:, slot, :], iota_row[:, :], lo, meta(2, i * 8 + slot, 1), ALU.is_equal, ALU.mult)
                else:
                    ins = v.tensor_scalar(S[:, slot, :], iota_row[:, :], lo, None, ALU.is_equal)
                if u == HALF - 1:
                    ins.then_inc(s_ready, 1)

            def add(p, i, h, u, b, width):
                dve.wait_ge(agg_added, i * 8 + (TILES * turn(p) + HALF * h + u + 8))
                v.tensor_tensor(AGG[:, ds(b[HALF * h + u], 1), 0:width].rearrange("p b f -> p (b f)"),
                                AGG[:, ds(b[HALF * h + u], 1), 0:width].rearrange("p b f -> p (b f)"),
                                seg_bank[h][:, u * P:u * P + width], ALU.add).then_inc(agg_added, 1)

            def hots_and_adds(p, hot, add_, b, width):
                if hot:
                    dve.wait_ge(seg_done, hot[0] * 2 + (HALVES * turn(p) + hot[1] + 1))
                if add_:
                    dve.wait_ge(seg_done, add_[0] * 2 + (HALVES * turn(p) + add_[1] + 3))
                for u in range(HALF):
                    if add_:
                        add(p, add_[0], add_[1], u, b, width)
                    if hot:
                        one_hot(p, hot[0], hot[1], u)

            def z_add(i, h):
                dve.wait_ge(s_g[0][h], i * 64 + 64)
                dve.wait_ge(z_mm, i * 2 + h + 3)
                if not isinstance(i, int):
                    dve.wait_ge(h_ready, i * 2 + h - 1)
                for k in range(2):
                    sl = slice(HALF * h + 2 * k, HALF * h + 2 * k + 2)
                    last = v.tensor_tensor(Z[:, sl, :], G[:, sl, :], z_bank[h][k][:, 0:384].rearrange("p (t f) -> p t f", t=2), ALU.add)
                last.then_inc(z_added, 1)

            def gate_lin(i, h):
                dve.wait_ge(h_ready, i * 2 + h + 1)
                sl = slice(HALF * h, HALF * h + HALF)
                if not (isinstance(i, int) and i == 0 and h == 0):
                    dve.wait_ge(lin_ready, i * 2 + h)
                v.tensor_tensor(prod[:, :, :], H[:, sl, 0:F], gw2[:, :].unsqueeze(1).to_broadcast([P, HALF, F]), ALU.mult).then_inc(prod_ready, 1)
                dve.wait_ge(prod_ready, i * 2 + h + 1)
                v.reduce_sum(glin[:, sl], prod[:, :, :], axis=AX.X).then_inc(lin_ready, 1)

            def gated(i, h):
                dve.wait_ge(th_ready, i * 2 + h + 1)
                sl = slice(HALF * h, HALF * h + HALF)
                v.tensor_scalar(gate[:, sl], gth[:, sl], 0.5, 0.5, ALU.mult, ALU.add).then_inc(gate_ready, 1)
                dve.wait_ge(gate_ready, i * 2 + h + 1)
                dve.wait_ge(seg_done, i * 2 + h + 1)
                v.tensor_tensor(M[:, sl, 0:F + 1], H[:, sl, F:2 * F + 1],
                                gate[:, sl].unsqueeze(2).to_broadcast([P, HALF, F + 1]), ALU.mult).then_inc(m_ready, 1)

            z_add(0, 0)
            z_add(0, 1)
            gate_lin(0, 0)
            hots_and_adds(0, (0, 0), None, None, MW)
            gated(0, 0)
            with dve.Fori(1, PAIRS) as i:
                b = blocks(i * 8 - 8)
                z_add(i, 0)
                gate_lin(i - 1, 1)
                hots_and_adds(0, (i - 1, 1), (i - 1, 0), b, MW)
                gated(i - 1, 1)
                z_add(i, 1)
                gate_lin(i, 0)
                hots_and_adds(0, (i, 0), (i - 1, 1), b, MW)
                gated(i, 0)
            L = PAIRS - 1
            gate_lin(L, 1)
            b = blocks(L * 8)
            hots_and_adds(0, (L, 1), (L, 0), b, MW)
            gated(L, 1)
            hots_and_adds(0, None, (L, 1), b, MW)
            dve.wait_ge(agg_added, TILES + 8)
            dve.wait_ge(th_ready, HALVES)
            v.memset(Hf[F:F + 1, 0:512], 1.0).then_inc(ones_row, 1)
            step(v.tensor_scalar(deg[:, :], AGG[:, :, MW - 1:MW].rearrange("p b f -> p (b f)"), 1.0, None, ALU.add))
            dve.engine_nop().then_inc(pass_done, 1)

            with dve.Fori(0, CHUNKS) as c:
                dve.wait_ge(p_tr, c + 2)
                dve.wait_ge(p_u, c + 1)
                v.tensor_copy(XT[0:F, :], PS[3][0:F, :]).then_inc(x_ev, 1)
                dve.wait_ge(p_gt, c + 2)
                v.tensor_copy(GT, PS[4][0:F, :]).then_inc(g_ev, 1)
                dve.wait_ge(p_up, c + 2)
                v.tensor_tensor(AGG[:, ds(c * CH, CH), 0:F], X[:, ds(c * CH, CH), :],
                                PS[6][:, 0:CH * F].rearrange("p (k f) -> p k f", k=CH), ALU.add).then_inc(h_done, 1)
            dve.wait_ge(h_done, CHUNKS + 1)

            sqrts = [0]

            def root():
                sqrts[0] += 1
                dve.engine_nop().then_inc(var_ready, 1)
                dve.wait_ge(act_sqrt, sqrts[0])

            def wide(x):
                return x.unsqueeze(2).to_broadcast([P, NB, F])

            def per_feature(x):
                return x.unsqueeze(1).to_broadcast([P, NB, F])

            def layernorm(Y, square):
                mean, var, std = stat[:, 0, :], stat[:, 1, :], stat[:, 2, :]
                step(v.reduce_sum(mean, Y, axis=AX.X))
                step(v.tensor_scalar(mean, mean, 1.0 / F, None, ALU.mult))
                step(v.tensor_tensor(Y, Y, wide(mean), ALU.subtract))
                step(v.tensor_tensor(square, Y, Y, ALU.mult))
                step(v.reduce_sum(var, square, axis=AX.X))
                root()
                step(v.reciprocal(std, std))
                step(v.tensor_tensor(Y, Y, wide(std), ALU.mult))

            Xa = X[:, :, :]
            layernorm(Af, TX)
            step(v.tensor_tensor(Af, Af, per_feature(lng[:, :]), ALU.mult))
            step(v.tensor_tensor(Af, Af, per_feature(lnb[:, :]), ALU.add))
            step(v.tensor_tensor(Xa, Xa, Af, ALU.add))
            layernorm(Xa, TX)
            dve.engine_nop().then_inc(x_ready, 1)

            def hots_and_diags(i, h, again):
                if again:
                    dve.wait_ge(ct_done, i * 2 + h + 1)
                    dve.wait_ge(bc_done, i * 2 + h + 1)
                for u in range(HALF):
                    slot = HALF * h + u
                    last = v.tensor_scalar(DIAG[:, slot, :], ident[:, :], meta(0, i * 8 + slot, 1), None, ALU.mult)
                last.then_inc(diag_ready, 1)
                for u in range(HALF):
                    slot = HALF * h + u
                    last = v.tensor_scalar(S[:, slot, :], iota_row[:, :], meta(1, i * 8 + slot, 1), meta(2, i * 8 + slot, 1),
                                           ALU.is_equal, ALU.mult)

            def same_and_places(i, h, again):
                J = i * 2 + h
                sl = slice(HALF * h, HALF * h + HALF)
                dve.wait_ge(bc_done, J + 3)
                dve.wait_ge(ct_done, J + 1)
                v.tensor_tensor(SAME[:, sl, :], PS[h][:, :].rearrange("p (t e) -> p t e", e=P),
                                meta(0, i * 8 + HALF * h, HALF).unsqueeze(2).to_broadcast([P, HALF, P]), ALU.is_equal).then_inc(same_ready, 1)
                dve.wait_ge(same_ready, J + 3)
                v.tensor_scalar(from_spare[:, sl], meta(0, i * 8 + HALF * h, HALF), spare[:, 0:1], None, ALU.subtract)
                for u in range(HALF):
                    slot = HALF * h + u
                    last = v.tensor_tensor_reduce(out=DIAG[:, slot, :], in0=SAME[:, slot, :], in1=earlier[:, :], scale=1.0, scalar=0.0,
                                                  op0=ALU.mult, op1=ALU.add, accum_out=repeats[:, slot:slot + 1])
                last.then_inc(rep_done, 1)
                dve.wait_ge(rep_done, J + 1)
                v.scalar_tensor_tensor(first[:, sl], repeats[:, sl], 0.0, from_spare[:, sl], ALU.is_equal, ALU.mult).then_inc(first_done, 1)
                dve.wait_ge(first_done, J + 1)
                if again:
                    for u in range(HALF * h, HALF * h + HALF):
                        dve.wait_ge(s_sc[u], i * 16)
                v.tensor_scalar(idx_st[:, sl], first[:, sl], spare[:, 0:1], None, ALU.add).then_inc(sc_idx, 1)

            dve.wait_ge(idx_staged, STAGES)
            hots_and_diags(0, 0, False)
            hots_and_diags(0, 1, False)
            same_and_places(0, 0, False)
            hots_and_diags(1, 0, True)
            same_and_places(0, 1, False)
            with dve.Fori(1, PAIRS - 1) as i:
                hots_and_diags(i, 1, True)
                same_and_places(i, 0, True)
                hots_and_diags(i + 1, 0, True)
                same_and_places(i, 1, True)
            hots_and_diags(PAIRS - 1, 1, True)
            same_and_places(PAIRS - 1, 0, True)
            same_and_places(PAIRS - 1, 1, True)
            for k in range(COPIES):
                dve.wait_ge(s_back[k % 2], 16 * (k // 2 + 1))
                v.tensor_tensor(Xa, Xa, (Af, TX)[k % 2], ALU.add).then_inc(copy_added, 1)
                dve.wait_ge(copy_added, k + 1)

            def tile_pass(p):
                dve.wait_ge(agg_zero, p - 1)
                hots_and_adds(p, (0, 0), None, None, F)
                with dve.Fori(0, PAIRS - 1) as i:
                    b = blocks(i * 8)
                    hots_and_adds(p, (i, 1), (i, 0), b, F)
                    hots_and_adds(p, (i + 1, 0), (i, 1), b, F)
                b = blocks((PAIRS - 1) * 8)
                hots_and_adds(p, (PAIRS - 1, 1), (PAIRS - 1, 0), b, F)
                hots_and_adds(p, None, (PAIRS - 1, 1), b, F)
                dve.wait_ge(agg_added, TILES * (turn(p) + 1) + 8)

            layernorm(Xa, TX)
            root()
            step(v.reciprocal(dinv[:, :], stat[:, 2, :]))
            root()
            step(v.reciprocal(vec[:, 6:7], vec[:, 6:7]))
            step(v.tensor_tensor(vec[:, 6:7], vec[:, 6:7], vec[:, 2:3], ALU.mult))
            step(v.tensor_tensor(vec[:, 7:8], vec[:, 6:7], vec[:, 4:5], ALU.mult))
            step(v.tensor_tensor(vec[:, 7:8], vec[:, 3:4], vec[:, 7:8], ALU.subtract))
            step(v.tensor_tensor(TX, Xa, wide(dinv[:, :]), ALU.mult))
            dve.engine_nop().then_inc(x_ready, 1)
            tile_pass(2)
            step(v.tensor_tensor(Af, Af, TX, ALU.add))
            step(v.tensor_tensor(Af, Af, wide(dinv[:, :]), ALU.mult))
            dve.engine_nop().then_inc(pass_done, 1)
            with dve.Fori(0, CHUNKS) as c:
                dve.wait_ge(z2_ev, c + 2)
                dve.wait_ge(bn_ready, c + 1)
                v.scalar_tensor_tensor(XT[0:F, :], GT, 0.05, GT, ALU.mult, ALU.max).then_inc(lk_done, 1)
                dve.wait_ge(lk_done, c + 2)
                dve.wait_ge(p_up, c + CHUNKS + 1)
                v.tensor_scalar(YT, XT[0:F, :], vec[:, 6:7], vec[:, 7:8], ALU.mult, ALU.add).then_inc(bn_ready, 1)
                dve.wait_ge(p_up, c + CHUNKS + 2)
                v.tensor_tensor(TX[:, ds(c * CH, CH), :], PS[6][:, 0:CH * F].rearrange("p (k f) -> p k f", k=CH),
                                dinv[:, ds(c * CH, CH)].unsqueeze(2).to_broadcast([P, CH, F]), ALU.mult).then_inc(h_done, 1)
            dve.wait_ge(h_done, 2 * CHUNKS + 1)
            dve.engine_nop().then_inc(x_ready, 1)
            tile_pass(3)
            step(v.tensor_tensor(Af, Af, TX, ALU.add))
            step(v.tensor_tensor(Af, Af, wide(dinv[:, :]), ALU.mult))
            step(v.tensor_tensor(Af, Af, per_feature(b2r[:, :]), ALU.add))
            dve.engine_nop().then_inc(pass_done, 1)
            step(v.tensor_tensor(Xa, Xa, Af, ALU.add))
            layernorm(Xa, TX)
            dve.engine_nop().then_inc(x_ready, 1)
            tile_pass(4)
            v.memset(Zf[F:F + 1, 512:1024], 1.0).then_inc(ones_row, 1)
            dve.engine_nop().then_inc(pass_done, 1)
            with dve.Fori(0, CHUNKS) as c:
                dve.wait_ge(p_tr, c + 2 * CHUNKS + 2)
                dve.wait_ge(p_up, c + 2 * CHUNKS + 1)
                v.tensor_copy(XT[0:F, :], PS[3][0:F, :]).then_inc(x_ev, 1)
                dve.wait_ge(p_up, c + 2 * CHUNKS + 2)
                v.tensor_copy(AGG[:, ds(c * CH, CH), 0:F], PS[6][:, 0:CH * F].rearrange("p (k f) -> p k f", k=CH)).then_inc(h_done, 1)
            dve.wait_ge(h_done, 3 * CHUNKS + 1)
            step(v.tensor_tensor(Xa, Xa, Af, ALU.add))
            layernorm(Xa, TX)
            dve.engine_nop().then_inc(x_ready, 1)


NAMES = {
    "mW1": "L0_gnn_mW1", "mb1": "L0_gnn_mb1", "mW2": "L0_gnn_mW2", "mb2": "L0_gnn_mb2",
    "gW1": "L0_gnn_gW1", "gb1": "L0_gnn_gb1", "gW2": "L0_gnn_gW2", "gb2": "L0_gnn_gb2",
    "uW1": "L0_gnn_uW1", "ub1": "L0_gnn_ub1", "uW2": "L0_gnn_uW2", "ub2": "L0_gnn_ub2",
    "ln_g": "L0_gnn_ln_g", "ln_b": "L0_gnn_ln_b", "W1": "L2_gnn_W1", "b1": "L2_gnn_b1",
    "W2": "L2_gnn_W2", "b2": "L2_gnn_b2", "bn_gamma": "L2_gnn_bn_gamma", "bn_beta": "L2_gnn_bn_beta",
    "bn_mean": "L2_gnn_bn_mean", "bn_var": "L2_gnn_bn_var", "mlp_b": "L3_gnn_mlp_b",
}


def kernel(**inputs):
    import numpy as np
    import concourse.bacc as bacc
    from concourse.bass_utils import run_bass_kernel_spmd

    def padded(v, fill):
        v = np.asarray(v)
        return np.concatenate([v, np.full((EPAD - E,), fill, v.dtype)])

    x = np.zeros((NPAD, F), np.asarray(inputs["x"]).dtype)
    x[:N] = inputs["x"]
    xT = x.T
    ea = np.asarray(inputs["edge_attr_32"])
    eaT = np.zeros((EF, EPAD), ea.dtype)
    eaT[:, :E] = ea.T
    host = {
        "x": x.reshape(NB, P, F).transpose(1, 0, 2), "xT": xT, "eaT": eaT,
        "src": padded(inputs["src"], NREAL * P), "dst": padded(inputs["dst"], NREAL * P),
        "w": padded(inputs["edge_weight"], 0), "mlp_wT": np.asarray(inputs["L3_gnn_mlp_w"]).T,
    }
    for short, name in NAMES.items():
        host[short] = np.asarray(inputs[name])
    nc = bacc.Bacc("TRN2", target_bir_lowering=False, num_devices=1)
    arrays, aps = {}, {}
    for name, v in host.items():
        v = np.ascontiguousarray(v)
        arrays[f"in_{name}"] = v
        aps[name] = nc.dram_tensor(f"in_{name}", v.shape, mybir.dt.from_np(v.dtype), kind="ExternalInput").ap()
    out = nc.dram_tensor("out", (P, NB, F), mybir.dt.float32, kind="ExternalOutput").ap()
    build(nc, aps, out)
    r = run_bass_kernel_spmd(nc, [arrays], core_ids=[0])
    return np.ascontiguousarray(r.results[0]["out"].transpose(1, 0, 2).reshape(NPAD, F)[:N])
```

```python
import concourse.bass as bass
from concourse import mybir
from contextlib import ExitStack

N = 12500
F = 96
EF = 32
E = 200000
P = 128
EPS = 1e-5

NB = 100
NREAL = -(-N // P)
NPAD = NB * P
BINS = NREAL + 1
T0_SLOTS = 5
T0_ROUNDS = NB // (2 * T0_SLOTS)
BINS_DVE = BINS - (T0_SLOTS + 1) * T0_ROUNDS
BINS_ROUND = 3
COPIES = 8

TPM = 1568
EPAD = P * TPM
TILES = 1664
assert (E + 127 * NREAL) // P <= TILES and TILES % P == 0 and EPAD - E >= P and TPM % 8 == 0
TCH = TILES // P
TCOL = TILES + 8
HALF = 4
HALVES = TILES // HALF
PAIRS = HALVES // 2
ZERO_ROWS = 4 * P
COPY_ROWS = PAIRS // COPIES * ZERO_ROWS
assert PAIRS % COPIES == 0 and COPY_ROWS >= NPAD + P
STAGES = HALVES + 2
MW = 98
CH = 4
CHUNKS = NB // CH
GB = 10
GROUPS = NB // GB


def build(nc, a, out):
    f32, i32, bf16 = mybir.dt.float32, mybir.dt.int32, mybir.dt.bfloat16
    ALU = mybir.AluOpType
    ACT = mybir.ActivationFunctionType
    AX = mybir.AxisListType
    DVE = mybir.EngineType.DVE
    SPE = mybir.EngineType.SP
    ds = bass.ds
    ctx = ExitStack()
    with ctx:
        def sb(name, shape, dt=f32):
            return ctx.enter_context(nc.sbuf_tensor(name, shape, dt))

        def sem(name):
            return ctx.enter_context(nc.semaphore(name))

        table0 = nc.dram_tensor("table0", (NPAD, 2 * F), f32).ap()
        table = {i: nc.dram_tensor(f"table{i}", (NPAD, F), f32).ap() for i in (2, 3, 4)}
        copy = [nc.dram_tensor(f"copy{i}", (COPY_ROWS, F), f32).ap() for i in range(COPIES)]
        tile_dram = nc.dram_tensor("tile_dram", (2 * TCH, P), i32).ap()

        X = sb("X", [P, NB, F])
        AGG = sb("AGG", [P, NB, MW])
        BIG = sb("BIG", [P, NB * F])
        MD = sb("MD", [P, 3, TCOL])
        tile_row = sb("tile_row", [1, 2 * TILES], i32)
        G = sb("G", [P, 8, 2 * F])
        Z = sb("Z", [P, 8, 2 * F])
        H = sb("H", [P, 8, 2 * F + 1])
        M = sb("M", [P, 8, MW])
        S = sb("S", [P, 8, P])
        CT = sb("CT", [P, 8, P])
        EA = CT[0:EF, :, :]
        zeros = sb("zeros", [P, ZERO_ROWS // P * F])
        prod = sb("prod", [P, HALF, F])
        idx_st = sb("idx_st", [P, 8], i32)
        glin = sb("glin", [P, 8])
        gth = sb("gth", [P, 8])
        gate = sb("gate", [P, 8])
        iota_row = sb("iota_row", [P, P])
        iota_i = sb("iota_i", [P, P], i32)
        tile_id = sb("tile_id", [P, TCH])
        tile_id_i = sb("tile_id_i", [P, TCH], i32)
        part_i = sb("part_i", [P, P], i32)
        ident = sb("ident", [P, P])
        earlier = sb("earlier", [P, P])
        ones = sb("ones", [P, P])
        cnt = sb("cnt", [P, BINS])
        minus_bin = sb("minus_bin", [P, P])
        row_f = sb("row_f", [P, 5, BINS])
        row_i = sb("row_i", [P, 2, BINS], i32)
        junk = sb("junk", [P, 2, BINS])
        tcol = sb("tcol", [P, 3, TCH])
        repeats = sb("repeats", [P, 8])
        first = sb("first", [P, 8])
        spare = sb("spare", [P, 1])
        spare_i = sb("spare_i", [P, 1], i32)
        from_spare = sb("from_spare", [P, 8])
        tcol_i = sb("tcol_i", [P, TCH], i32)
        tp_i = sb("tp_i", [2 * TCH, P], i32)
        stat = sb("stat", [P, 3, NB])
        deg = sb("deg", [P, NB])
        dinv = sb("dinv", [P, NB])
        W0 = sb("W0", [F + 1, 2 * F])
        WE = sb("WE", [EF, 2 * F])
        gw2 = sb("gw2", [P, F])
        gb2 = sb("gb2", [P, 1])
        half = sb("half", [P, 1])
        hgb2 = sb("hgb2", [P, 1])
        W2a = sb("W2a", [F + 1, F])
        U1x = sb("U1x", [F, F])
        U1g = sb("U1g", [F, F])
        W2T = sb("W2T", [F, F + 1])
        WU = sb("WU", [F + 1, F])
        U2 = sb("U2", [F + 1, F])
        lng = sb("lng", [P, F])
        lnb = sb("lnb", [P, F])
        C1 = sb("C1", [F, F])
        C2 = sb("C2", [F, F])
        b2r = sb("b2r", [P, F])
        L3x = sb("L3x", [F + 1, F])
        L3g = sb("L3g", [F, F])
        vec = sb("vec", [F, 8])
        eps = sb("eps", [P, 1])
        Gf = G[:, :, :].rearrange("p a b -> p (a b)")
        Zf = Z[:, :, :].rearrange("p a b -> p (a b)")
        Hf = H[:, :, :].rearrange("p a b -> p (a b)")
        AS = Gf[:, 0:CH * 97].rearrange("p (k f) -> p k f", k=CH)
        XS = Gf[:, 512:512 + CH * F].rearrange("p (k f) -> p k f", k=CH)
        AT = Zf[0:F + 1, 0:CH * P]
        XT = Zf[0:F + 1, 512:1024]
        GT = Zf[0:F, 1024:1536]
        UT = Hf[0:F + 1, 0:512]
        YT = Hf[0:F, 512:1024]
        DIAG = Zf[:, 0:8 * P].rearrange("p (t e) -> p t e", e=P)
        SAME = Hf[:, 0:8 * P].rearrange("p (t e) -> p t e", e=P)
        EARLY = M[:, :, :].rearrange("p a b -> p (a b)")[:, 0:HALF * P].rearrange("p (t e) -> p t e", e=P)
        MSG = Gf[:, 0:8 * F].rearrange("p (t f) -> p t f", f=F)
        pm_dst = BIG[:, 0:TPM].bitcast(i32)
        hi_i = BIG[:, TPM:2 * TPM].bitcast(i32)
        hi_f = BIG[:, 2 * TPM:2 * TPM + TPM // 2].bitcast(bf16)
        hjunk_act = BIG[:, 4 * TPM:4 * TPM + TPM // 2].bitcast(bf16)
        hjunk = BIG[:, 3 * TPM:3 * TPM + TPM // 2].bitcast(bf16)
        ROWS = BIG[:, 0:3 * TCH * P].rearrange("p (k c e) -> p k c e", k=3, e=P)
        ROWI = BIG[:, 3 * TCH * P:5 * TCH * P].bitcast(i32).rearrange("p (k c e) -> p k c e", k=2, e=P)
        AC = AGG[:, :, :].rearrange("p b f -> p (b f)")[:, 0:NB * F].rearrange("p (b f) -> p b f", f=F)
        TX = BIG[:, :].rearrange("p (b f) -> p b f", f=F)
        T0X = [Zf[0:F + 1, j * 2 * P:(j + 1) * 2 * P] for j in range(T0_SLOTS)]
        T0S = [Gf[:, j * 4 * F:(j + 1) * 4 * F] for j in range(T0_SLOTS - 1)] + [BIG[:, NB * F - 4 * F:]]

        LOADS = 28

        PS = [ctx.enter_context(nc.psum_tensor(f"bank{i}", [P, 512], f32)) for i in range(8)]
        seg_bank = [PS[0], PS[1]]
        z_bank = [[PS[2], PS[3]], [PS[4], PS[5]]]
        t0_bank = PS[1:1 + T0_SLOTS]

        s_load = sem("s_load")
        s_pm = sem("s_pm")
        const_ready = sem("const_ready")
        dve_step = sem("dve_step")
        act_step = sem("act_step")
        cnt_ready = sem("cnt_ready")
        tot_ready = sem("tot_ready")
        tiles_known = sem("tiles_known")
        tcol_t = sem("tcol_t")
        trow_out = sem("trow_out")
        s_trow = sem("s_trow")
        s_rows = [sem(f"s_rows{k}") for k in range(3)]
        rows_f = sem("rows_f")
        rows_t = sem("rows_t")
        md_ready = sem("md_ready")
        s_x = sem("s_x")
        s_xt = [sem(f"s_xt{j}") for j in range(T0_SLOTS)]
        t0_mm = sem("t0_mm")
        t0_ev = sem("t0_ev")
        s_t0 = [sem(f"s_t0{j}") for j in range(T0_SLOTS)]
        s_xc = sem("s_xc")
        idx_two = sem("idx_two")
        idx_staged = sem("idx_staged")
        s_two = [[sem(f"s_two{h}_{k}") for k in range(2)] for h in range(2)]
        s_g = {p: [sem(f"s_g{p}_{h}") for h in range(2)] for p in (2, 3, 4)}
        s_ea = [sem("s_ea0"), sem("s_ea1")]
        z_mm = sem("z_mm")
        z_added = sem("z_added")
        h_ready = sem("h_ready")
        lin_ready = sem("lin_ready")
        th_ready = sem("th_ready")
        gate_ready = sem("gate_ready")
        m_ready = sem("m_ready")
        s_ready = sem("s_ready")
        seg_done = sem("seg_done")
        agg_added = sem("agg_added")
        pass_done = sem("pass_done")
        a_staged = sem("a_staged")
        x_staged = sem("x_staged")
        p_at = sem("p_at")
        p_xt = sem("p_xt")
        a_ev = sem("a_ev")
        x_ev = sem("x_ev")
        fold_mm = sem("fold_mm")
        fold_ev = sem("fold_ev")
        p_gt = sem("p_gt")
        p_u = sem("p_u")
        u_ev = sem("u_ev")
        p_up = sem("p_up")
        h_done = sem("h_done")
        ln_step = sem("ln_step")
        centred = sem("centred")
        squared = sem("squared")
        var_ready = sem("var_ready")
        root_ready = sem("root_ready")
        scale_ready = sem("scale_ready")
        normed = sem("normed")
        scaled = sem("scaled")
        s_zero = sem("s_zero")
        diag_ready = sem("diag_ready")
        bc_done = sem("bc_done")
        same_ready = sem("same_ready")
        ct_done = sem("ct_done")
        ct_ev = sem("ct_ev")
        msg_done = sem("msg_done")
        msg_ev = sem("msg_ev")
        rep_done = sem("rep_done")
        first_done = sem("first_done")
        sc_idx = sem("sc_idx")
        s_sc = [sem(f"s_sc{u}") for u in range(COPIES)]
        s_back = [[sem(f"s_back{k}_{q}") for q in range(2)] for k in range(2)]
        copy_added = sem("copy_added")
        x_ready = sem("x_ready")
        agg_set = sem("agg_set")
        s_table = sem("s_table")
        s_out = sem("s_out")
        ones_row = sem("ones_row")
        hi_ready = sem("hi_ready")
        sgn_done = sem("sgn_done")
        hist_step = sem("hist_step")
        z2_ev = sem("z2_ev")
        lk_done = sem("lk_done")
        bn_ready = sem("bn_ready")
        block = ctx.enter_context(nc.Block())

        def chain(eng, semaphore):
            count = [0]

            def step(ins):
                count[0] += 1
                ins.then_inc(semaphore, 1)
                eng.wait_ge(semaphore, count[0])
            return step

        def table_view(ap):
            return ap.rearrange("(p b) f -> p b f", p=P)

        def meta(k, t0, n):
            return MD[:, k, ds(t0, n)]

        def skewed(eng, total, parts):
            lags = max(lag for _, lag in parts)

            def round_(c):
                for part, lag in parts:
                    if not isinstance(c, int) or 0 <= c - lag < total:
                        part(c - lag)

            for c in range(lags):
                round_(c)
            with eng.Fori(lags, total) as c:
                round_(c)
            for c in range(total, total + lags):
                round_(c)

        def turn(p):
            return p if p == 0 else p - 1

        TABLE_PARTS = {2: 16 * GROUPS, 3: 16 * (GROUPS + CHUNKS // 5), 4: 16 * (2 * GROUPS + CHUNKS // 5)}
        AGG_PARTS = {2: GROUPS, 3: GROUPS + CHUNKS, 4: 2 * GROUPS + CHUNKS}
        WEIGHTED = (False, True, False, False, True)

        @block.sync
        def _(sp):
            sp.dma_start(pm_dst, a["dst"].rearrange("(p t) -> p t", p=P)).then_inc(s_pm, 16)
            loads = [
                (W0[0:F, 0:F], a["gW1"][0:F, :]), (W0[0:F, F:2 * F], a["mW1"][0:F, :]),
                (W0[F:F + 1, 0:F], a["gb1"].unsqueeze(0)), (W0[F:F + 1, F:2 * F], a["mb1"].unsqueeze(0)),
                (WE[:, 0:F], a["gW1"][F:F + EF, :]), (WE[:, F:2 * F], a["mW1"][F:F + EF, :]),
                (gw2[:, :], a["gW2"].rearrange("f a -> (a f)").partition_broadcast(P)),
                (gb2[:, :], a["gb2"].partition_broadcast(P)),
                (W2a[0:F, :], a["mW2"]), (W2a[F:F + 1, :], a["mb2"].unsqueeze(0)),
                (U1x[:, :], a["uW1"][0:F, :]), (U1g[:, :], a["uW1"][F:2 * F, :]),
                (U2[0:F, :], a["uW2"]), (U2[F:F + 1, :], a["ub2"].unsqueeze(0)),
                (lng[:, :], a["ln_g"].partition_broadcast(P)), (lnb[:, :], a["ln_b"].partition_broadcast(P)),
                (C1[:, :], a["W1"]), (C2[:, :], a["W2"]), (b2r[:, :], a["b2"].partition_broadcast(P)),
                (L3x[0:F, :], a["mlp_wT"][0:F, :]), (L3x[F:F + 1, :], a["mlp_b"].unsqueeze(0)),
                (L3g[:, :], a["mlp_wT"][F:2 * F, :]),
            ] + [(vec[:, i:i + 1], a[n].unsqueeze(1)) for i, n in enumerate(("ub1", "b1", "bn_gamma", "bn_beta", "bn_mean", "bn_var"))]
            for o, i in loads:
                sp.dma_start(o, i).then_inc(s_load, 16)
            assert len(loads) == LOADS
            with sp.Fori(0, T0_ROUNDS) as i:
                for j in range(T0_SLOTS):
                    sp.wait_ge(t0_mm, i * T0_SLOTS + j + 1)
                    sp.nop(nofuse=True)
                    sp.dma_start(T0X[j][0:F, :], a["xT"][:, ds(i * (T0_SLOTS * 2 * P) + j * 2 * P, 2 * P)]).then_inc(s_xt[j], 16)
            sp.dma_start(X[:, :, :], a["x"]).then_inc(s_x, 16)
            sp.wait_ge(trow_out, 1)
            sp.dma_start(tile_dram, tp_i[:, :]).then_inc(s_trow, 16)
            sp.wait_ge(s_trow, 16)
            sp.dma_start(tile_row[0:1, :], tile_dram.rearrange("(o c) p -> o (c p)", o=1)).then_inc(s_trow, 16)
            sp.wait_ge(s_trow, 32)
            sp.wait_ge(const_ready, 12)

            def edge_features(i):
                _, first = nc.values_load_multi_w_load_instructions(
                    tile_row[0:1, ds(i * 8 + TILES, 8)], engines=[SPE], min_val=0, max_val=EPAD - P,
                    skip_runtime_bounds_check_because="DVE clamps the first edge to EPAD - 128")
                for h in range(2):
                    sp.wait_ge(z_mm, i * 2 + h + 1)
                    sp.nop(nofuse=True)
                    for u in range(HALF):
                        sp.dma_start(EA[:, HALF * h + u, :], a["eaT"][:, ds(first[HALF * h + u], P)]).then_inc(s_ea[h], 16)
            for k in range(COPIES):
                with sp.Fori(0, PAIRS // COPIES) as i:
                    edge_features(i + k * (PAIRS // COPIES))
                    sp.dma_start(copy[k][ds(i * ZERO_ROWS, ZERO_ROWS), :].rearrange("(p a) f -> p (a f)", p=P), zeros[:, :]).then_inc(s_zero, 16)
            sp.wait_ge(pass_done, 1)
            with sp.Fori(0, CHUNKS) as k:
                sp.wait_ge(p_u, k + 1)
                sp.nop(nofuse=True)
                sp.dma_start(XT[0:F, :], a["xT"][:, ds(k * (CH * P), CH * P)]).then_inc(s_xc, 16)
            for k in range(COPIES):
                sp.wait_ge(s_sc[k], 16 * PAIRS)
            for k in range(COPIES):
                for q in range(2):
                    if k >= 2:
                        sp.wait_ge(copy_added, 2 * (k - 2) + q + 1)
                    part = slice(q * NB // 2, (q + 1) * NB // 2)
                    sp.dma_start((AC, TX)[k % 2][:, part, :], table_view(copy[k][0:NPAD, :])[:, part, :]).then_inc(s_back[k % 2][q], 16)
            def leave(to, on_chip, ready, groups, chunks_each, base, signal):
                blocks_each = NB // groups
                with sp.Fori(0, groups) as g:
                    sp.wait_ge(ready, g * chunks_each + (base + chunks_each))
                    sp.nop(nofuse=True)
                    sp.dma_start(to[:, ds(g * blocks_each, blocks_each), :], on_chip[:, ds(g * blocks_each, blocks_each), :]).then_inc(signal, 16)

            leave(table_view(table[2]), TX, scaled, GROUPS, 1, 0, s_table)
            leave(table_view(table[3]), TX, h_done, CHUNKS // 5, 5, CHUNKS + 1, s_table)
            leave(table_view(table[4]), X, normed, GROUPS, 1, 2 * GROUPS, s_table)
            leave(out, X, normed, CHUNKS // 5, 5, 3 * GROUPS, s_out)
            sp.wait_ge(s_out, 16 * (CHUNKS // 5))

        @block.gpsimd
        def _(pool):
            pool.iota(iota_i[:, :], pattern=[[1, P]], base=0, channel_multiplier=0).then_inc(const_ready, 1)
            pool.iota(part_i[:, :], pattern=[[0, P]], base=0, channel_multiplier=1).then_inc(const_ready, 1)
            pool.iota(tile_id_i[:, :], pattern=[[P, TCH]], base=0, channel_multiplier=1).then_inc(const_ready, 1)
            pool.memset(ones[:, :], 1.0).then_inc(const_ready, 1)
            pool.memset(H[:, :, 2 * F:2 * F + 1], 1.0).then_inc(const_ready, 1)
            pool.memset(M[:, :, MW - 1:MW], 1.0).then_inc(const_ready, 1)
            pool.memset(zeros[:, :], 0.0).then_inc(const_ready, 1)
            pool.memset(AGG[:, :, :], 0.0).then_inc(const_ready, 1)
            pool.iota(spare_i[:, :], pattern=[[0, 1]], base=NPAD, channel_multiplier=1).then_inc(const_ready, 1)
            pool.memset(MD[:, :, TILES:TCOL], 0.0).then_inc(const_ready, 1)
            pool.memset(eps[:, :], EPS).then_inc(const_ready, 1)
            pool.memset(half[:, :], 0.5).then_inc(const_ready, 1)
            pool.wait_ge(tiles_known, 1)
            pool.nop(nofuse=True)
            for k, n in enumerate(("src", "dst", "w")):
                for c in range(TCH):
                    o = ROWS[:, k, c, :] if k == 2 else ROWS[:, k, c, :].bitcast(i32)
                    pool.indirect_dma_start(out=o, out_offset=None, in_=a[n].rearrange("(n a) -> n a", a=1),
                                            in_offset=bass.IndirectOffsetOnAxis(ap=tcol_i[:, c:c + 1], axis=0)).then_inc(s_rows[k], 16)

            def gather(u, src_table, width):
                return pool.indirect_dma_start(out=G[:, u, 0:width], out_offset=None, in_=src_table,
                                               in_offset=bass.IndirectOffsetOnAxis(ap=idx_st[:, u:u + 1], axis=0))

            def gathers(p, src_table, width):
                with pool.Fori(0, PAIRS) as i:
                    for h in range(2):
                        pool.wait_ge(idx_staged, i * 2 + (STAGES * (p - 2) + h + 1))
                        pool.wait_ge(seg_done, i * 2 + (HALVES * turn(p) + h + 1))
                        pool.nop(nofuse=True)
                        for u in range(HALF * h, HALF * h + HALF):
                            gather(u, src_table, width).then_inc(s_g[p][h], 16)

            def stage_scaled(k):
                pool.wait_ge(p_at, k + CHUNKS + 1)
                pool.tensor_tensor(AS[:, :, 0:F], AGG[:, ds(k * CH, CH), 0:F],
                                   dinv[:, ds(k * CH, CH)].unsqueeze(2).to_broadcast([P, CH, F]), ALU.mult).then_inc(a_staged, 1)

            def stage_agg(first, width):
                def part(k):
                    pool.wait_ge(p_at, k + first + 1)
                    pool.tensor_copy(AS[:, :, 0:width], AGG[:, ds(k * CH, CH), 0:width]).then_inc(a_staged, 1)
                return part

            def stage_x(k):
                pool.wait_ge(p_xt, k + 1)
                pool.tensor_copy(XS[:, :, :], X[:, ds(k * CH, CH), :]).then_inc(x_staged, 1)

            for j in range(T0_SLOTS):
                pool.wait_ge(s_t0[j], 16 * T0_ROUNDS)
            pool.wait_ge(t0_mm, NB // 2 + T0_SLOTS)
            with pool.Fori(0, PAIRS) as i:
                for h in range(2):
                    for k in range(2):
                        pool.wait_ge(idx_two, i * 4 + (2 * h + k + 1))
                        pool.wait_ge(z_added, i * 4 + (2 * h + k + 1))
                        pool.nop(nofuse=True)
                        for u in (HALF * h + 2 * k, HALF * h + 2 * k + 1):
                            gather(u, table0, 2 * F).then_inc(s_two[h][k], 16)
            pool.wait_ge(pass_done, 1)
            skewed(pool, CHUNKS, [(stage_agg(0, F + 1), 0)])
            pool.wait_ge(s_zero, 16 * PAIRS)
            with pool.Fori(0, PAIRS) as i:
                for h in range(2):
                    pool.wait_ge(sc_idx, i * 2 + h + 1)
                    pool.wait_ge(msg_ev, i * 2 + h + 3)
                    pool.nop(nofuse=True)
                    for u in range(HALF * h, HALF * h + HALF):
                        pool.indirect_dma_start(
                            out=copy[u], out_offset=bass.IndirectOffsetOnAxis(ap=idx_st[:, u:u + 1], axis=0),
                            in_=MSG[:, u, :], in_offset=None, compute_op=ALU.add).then_inc(s_sc[u], 16)
            for p in (2, 3, 4):
                if p == 4:
                    for g in range(GROUPS):
                        pool.wait_ge(centred, g + (2 * GROUPS + 1))
                        pool.memset(AGG[:, g * GB:(g + 1) * GB, :], 0.0).then_inc(agg_set, 1)
                pool.wait_ge(s_table, TABLE_PARTS[p])
                gathers(p, table[p], F)
                pool.wait_ge(pass_done, p)
                if p == 2:
                    skewed(pool, CHUNKS, [(stage_scaled, 0)])
                if p == 4:
                    skewed(pool, CHUNKS, [(stage_agg(2 * CHUNKS, F), 0), (stage_x, 0)])

        @block.tensor
        def _(pe):
            mm = nc.tensor.matmul
            pe.sem_inc(t0_mm, T0_SLOTS)
            for s in (bc_done, ct_done, msg_done):
                pe.sem_inc(s, 2)
            pe.sem_inc(seg_done, 2)
            pe.sem_inc(z_mm, 2)
            for s in (p_at, p_xt, p_gt, p_u, p_up):
                pe.sem_inc(s, 1)
            pe.wait_ge(s_load, 16 * LOADS)
            pe.wait_ge(ones_row, 1)
            with pe.Fori(0, T0_ROUNDS) as i:
                for j in range(T0_SLOTS):
                    pe.wait_ge(s_xt[j], i * 16 + 16)
                    pe.wait_ge(t0_ev, i * T0_SLOTS + j + 1)
                    for k in range(2):
                        last = mm(t0_bank[j][:, k * 192:(k + 1) * 192], T0X[j][:, k * P:(k + 1) * P], W0[:, :], start=True, stop=True)
                    last.then_inc(t0_mm, 1)

            pe.wait_ge(t0_ev, NB // 2 + T0_SLOTS)
            nc.tensor.transpose(PS[2][0:F, 0:F + 1], W2a[:, :], ident[0:F + 1, 0:F + 1]).then_inc(fold_mm, 1)

            pe.wait_ge(cnt_ready, 1)
            pe.wait_ge(sgn_done, BINS - BINS_DVE + 1)
            mm(PS[6][:, 0:BINS], ones[:, :], cnt[:, :], start=True, stop=True).then_inc(tot_ready, 1)
            pe.wait_ge(fold_ev, 1)
            mm(PS[3][0:F + 1, 0:F], W2T[:, :], U1g[:, :], start=True, stop=True).then_inc(fold_mm, 1)
            pe.wait_ge(tiles_known, 1)
            nc.tensor.transpose(PS[7][0:2 * TCH, 0:P], tcol[:, 0:2, :].rearrange("p a c -> p (a c)"), ident[:, :]).then_inc(tcol_t, 1)
            for c in range(TCH):
                pe.wait_ge(rows_f, 1)
                if c >= 2:
                    pe.wait_ge(md_ready, c - 1)
                for k in range(3):
                    last = nc.tensor.transpose(seg_bank[c % 2][:, k * P:(k + 1) * P], ROWS[:, k, c, :], ident[:, :])
                last.then_inc(rows_t, 1)

            def z_half(i, h):
                pe.wait_ge(s_ea[h], i * 64 + 64)
                pe.wait_ge(z_added, i * 4 + 2 * h + 2)
                for u in range(HALF):
                    last = mm(z_bank[h][u // 2][:, (u % 2) * 192:(u % 2) * 192 + 192], EA[:, HALF * h + u, :], WE[:, :], start=True, stop=True)
                last.then_inc(z_mm, 1)

            def seg_half(p, i, h, width):
                if p == 0:
                    pe.wait_ge(m_ready, i * 2 + h + 1)
                else:
                    pe.wait_ge(s_g[p][h], i * 64 + 64)
                pe.wait_ge(s_ready, i * 2 + (HALVES * turn(p) + h + 1))
                pe.wait_ge(agg_added, i * 8 + (TILES * turn(p) + 4 * h + 4))
                for u in range(HALF):
                    rhs = M[:, HALF * h + u, :] if p == 0 else G[:, HALF * h + u, 0:F]
                    last = mm(seg_bank[h][:, u * P:u * P + width], S[:, HALF * h + u, :], rhs, start=True, stop=True)
                last.then_inc(seg_done, 1)

            pe.wait_ge(md_ready, TCH)
            z_half(0, 0)
            z_half(0, 1)
            z_half(1, 0)
            with pe.Fori(1, PAIRS - 1) as i:
                z_half(i, 1)
                seg_half(0, i - 1, 0, MW)
                z_half(i + 1, 0)
                seg_half(0, i - 1, 1, MW)
            z_half(PAIRS - 1, 1)
            seg_half(0, PAIRS - 2, 0, MW)
            seg_half(0, PAIRS - 2, 1, MW)
            seg_half(0, PAIRS - 1, 0, MW)
            seg_half(0, PAIRS - 1, 1, MW)

            def transpose_agg(first, width):
                def part(k):
                    pe.wait_ge(a_staged, k + first + 1)
                    pe.wait_ge(a_ev, k + first + 1)
                    for j in range(CH):
                        last = nc.tensor.transpose(PS[2][0:width, j * P:(j + 1) * P], AS[:, j, 0:width], ident[:, :])
                    last.then_inc(p_at, 1)
                return part

            def transpose_x(k):
                pe.wait_ge(x_staged, k + 1)
                pe.wait_ge(x_ev, k + 1)
                for j in range(CH):
                    last = nc.tensor.transpose(PS[3][0:F, j * P:(j + 1) * P], XS[:, j, :], ident[:, :])
                last.then_inc(p_xt, 1)

            def update_hidden(k):
                pe.wait_ge(a_ev, k + 2)
                pe.wait_ge(s_xc, k * 16 + 16)
                pe.wait_ge(u_ev, k + 1)
                mm(PS[5][0:F, :], U1x[:, :], XT[0:F, :], start=True, stop=False)
                mm(PS[5][0:F, :], WU[:, :], AT, start=False, stop=True).then_inc(p_u, 1)

            def update(k):
                pe.wait_ge(u_ev, k + 2)
                pe.wait_ge(h_done, k + 1)
                for j in range(CH):
                    last = mm(PS[6][:, j * F:(j + 1) * F], UT[:, j * P:(j + 1) * P], U2[:, :], start=True, stop=True)
                last.then_inc(p_up, 1)

            pe.wait_ge(ones_row, 2)
            skewed(pe, CHUNKS, [(update, 2), (update_hidden, 1), (transpose_agg(0, F + 1), 0)])

            def spread(i, h):
                pe.wait_ge(diag_ready, i * 2 + h + 1)
                pe.wait_ge(same_ready, i * 2 + h + 1)
                for u in range(HALF * h, HALF * h + HALF):
                    last = mm(PS[h][:, (u % HALF) * P:(u % HALF + 1) * P], ones[:, :], DIAG[:, u, :], start=True, stop=True)
                last.then_inc(bc_done, 1)

            def messages(i, h, b):
                pe.wait_ge(same_ready, i * 2 + h + 3)
                pe.wait_ge(ct_ev, i * 2 + h + 1)
                for u in range(HALF * h, HALF * h + HALF):
                    last = mm(PS[2 + h][:, (u % HALF) * P:(u % HALF + 1) * P], S[:, u, :], SAME[:, u, :], start=True, stop=True)
                last.then_inc(ct_done, 1)
                pe.wait_ge(ct_ev, i * 2 + h + 3)
                pe.wait_ge(msg_ev, i * 2 + h + 1)
                for u in range(HALF * h, HALF * h + HALF):
                    last = mm(PS[4 + h][:, (u % HALF) * F:(u % HALF + 1) * F], CT[:, u, :],
                              X[:, ds(b[u], 1), :].rearrange("p b f -> p (b f)"), start=True, stop=True)
                last.then_inc(msg_done, 1)

            def tile_blocks(i):
                _, b = nc.values_load_multi_w_load_instructions(
                    tile_row[0:1, ds(i * 8, 8)], engines=[mybir.EngineType.PE], min_val=0, max_val=NREAL,
                    skip_runtime_bounds_check_because="the block of a tile is clamped to NREAL when it is computed")
                return b

            pe.wait_ge(x_ready, 1)
            spread(0, 0)
            with pe.Fori(0, PAIRS - 1) as i:
                b = tile_blocks(i)
                spread(i, 1)
                messages(i, 0, b)
                spread(i + 1, 0)
                messages(i, 1, b)
            b = tile_blocks(PAIRS - 1)
            spread(PAIRS - 1, 1)
            messages(PAIRS - 1, 0, b)
            messages(PAIRS - 1, 1, b)

            def agg_pass(p):
                with pe.Fori(0, PAIRS) as i:
                    for h in range(2):
                        seg_half(p, i, h, F)

            agg_pass(2)
            def conv1(k):
                pe.wait_ge(a_ev, k + CHUNKS + 2)
                pe.wait_ge(z2_ev, k + 1)
                mm(PS[4][0:F, :], C1[:, :], AT[0:F, :], start=True, stop=True).then_inc(p_gt, 1)

            def conv2(k):
                pe.wait_ge(bn_ready, k + 2)
                pe.wait_ge(h_done, k + CHUNKS + 1)
                for j in range(CH):
                    last = mm(PS[6][:, j * F:(j + 1) * F], YT[:, j * P:(j + 1) * P], C2[:, :], start=True, stop=True)
                last.then_inc(p_up, 1)

            skewed(pe, CHUNKS, [(conv2, 2), (conv1, 1), (transpose_agg(CHUNKS, F), 0)])
            agg_pass(3)
            agg_pass(4)
            def output(k):
                pe.wait_ge(a_ev, k + 2 * CHUNKS + 2)
                pe.wait_ge(x_ev, k + 2)
                pe.wait_ge(h_done, k + 2 * CHUNKS + 1)
                for j in range(CH):
                    mm(PS[6][:, j * F:(j + 1) * F], XT[:, j * P:(j + 1) * P], L3x[:, :], start=True, stop=False)
                    last = mm(PS[6][:, j * F:(j + 1) * F], AT[0:F, j * P:(j + 1) * P], L3g[:, :], start=False, stop=True)
                last.then_inc(p_up, 1)

            pe.wait_ge(ones_row, 3)
            skewed(pe, CHUNKS, [(output, 1), (transpose_agg(2 * CHUNKS, F), 0), (transpose_x, 0)])

        @block.scalar
        def _(act):
            step = chain(act, act_step)
            act_fn = nc.scalar.activation
            act.sem_inc(sgn_done, 1)
            act.sem_inc(a_ev, 1)
            act.sem_inc(ct_ev, 2)
            act.sem_inc(msg_ev, 2)
            act.sem_inc(u_ev, 1)
            act.sem_inc(z2_ev, 1)

            def count_below(b):
                act_fn(hjunk_act, hi_f, ACT.Sign, bias=minus_bin[:, ds(b + BINS_DVE, 1)],
                       accum_out=cnt[:, ds(b + BINS_DVE, 1)]).then_inc(sgn_done, 1)

            act.wait_ge(hi_ready, 1)
            with act.Fori(0, T0_ROUNDS) as i:
                for j in range(T0_SLOTS):
                    act.wait_ge(t0_ev, i * T0_SLOTS + j + T0_SLOTS + 1)
                    act.dma_start(table_view(table0)[:, ds(i * 2 * T0_SLOTS + 2 * j, 2), :].rearrange("p b f -> p (b f)"), T0S[j]).then_inc(s_t0[j], 16)
                    act.wait_ge(sgn_done, i * (T0_SLOTS + 1) + j + 1)
                    count_below(i * (T0_SLOTS + 1) + j)
                act.wait_ge(sgn_done, i * (T0_SLOTS + 1) + T0_SLOTS + 1)
                count_below(i * (T0_SLOTS + 1) + T0_SLOTS)
            act.wait_ge(const_ready, 12)
            step(act_fn(hgb2[:, :], gb2[:, :], ACT.Copy, scale=0.5))

            def stage_two(i, h, k):
                act_fn(idx_st[:, HALF * h + 2 * k:HALF * h + 2 * k + 2], meta(0, i * 8 + HALF * h + 2 * k, 2), ACT.Copy).then_inc(idx_two, 1)

            def gelu(i, h):
                act.wait_ge(z_added, i * 4 + 2 * h + 6)
                if not isinstance(i, int):
                    act.wait_ge(lin_ready, i * 2 + h - 1)
                    act.wait_ge(m_ready, i * 2 + h - 1)
                act_fn(H[:, HALF * h:HALF * h + HALF, 0:2 * F], Z[:, HALF * h:HALF * h + HALF, :], ACT.Gelu).then_inc(h_ready, 1)

            def gated(i, h):
                sl = slice(HALF * h, HALF * h + HALF)
                act.wait_ge(lin_ready, i * 2 + h + 1)
                act_fn(gth[:, sl], glin[:, sl], ACT.Tanh, bias=hgb2[:, :], scale=0.5).then_inc(th_ready, 1)
                act.wait_ge(th_ready, i * 2 + h + 1)
                act_fn(gate[:, sl], gth[:, sl], ACT.Identity, bias=half[:, :], scale=0.5).then_inc(gate_ready, 1)
                act.wait_ge(gate_ready, i * 2 + h + 1)
                act.wait_ge(seg_done, i * 2 + h + 1)
                for u in range(HALF * h, HALF * h + HALF):
                    last = act_fn(M[:, u, 0:F + 1], H[:, u, F:2 * F + 1], ACT.Copy, scale=gate[:, u:u + 1])
                last.then_inc(m_ready, 1)

            act.wait_ge(md_ready, TCH)
            for h in range(2):
                for k in range(2):
                    stage_two(0, h, k)

            def stage_next(i, h):
                for k in range(2):
                    act.wait_ge(s_two[h][k], i * 32 + 32)
                    act.wait_ge(idx_two, i * 4 + 2 * h + k + 4)
                    stage_two(i + 1, h, k)

            stage_next(0, 0)
            gelu(0, 0)
            stage_next(0, 1)
            gelu(0, 1)
            gated(0, 0)
            with act.Fori(1, PAIRS) as i:
                stage_next(i, 0)
                gelu(i, 0)
                gated(i - 1, 1)
                stage_next(i, 1)
                gelu(i, 1)
                gated(i, 0)
            gated(PAIRS - 1, 1)

            def agg_copy(first, rows, freed, freed_first):
                def part(k):
                    act.wait_ge(p_at, k + first + 2)
                    act.wait_ge(freed, k + freed_first + 1)
                    act_fn(AT[0:rows, :], PS[2][0:rows, :], ACT.Copy).then_inc(a_ev, 1)
                return part

            def update_gelu(k):
                act.wait_ge(p_u, k + 2)
                act.wait_ge(p_up, k + 1)
                act_fn(UT[0:F, :], PS[5][0:F, :], ACT.Gelu, bias=vec[:, 0:1]).then_inc(u_ev, 1)

            def squares(Y, base, n):
                def part(k):
                    act.wait_ge(centred, k + (base + 1))
                    act_fn(TX[:, ds(k * n, n), :], Y[:, ds(k * n, n), 0:F], ACT.Square).then_inc(squared, 1)
                return part

            def self_loops(ready, base, n):
                def part(k):
                    act.wait_ge(ready, k + (base + 1))
                    act_fn(AGG[:, ds(k * n, n), 0:F], TX[:, ds(k * n, n), :], ACT.Copy).then_inc(agg_set, 1)
                return part

            def roots(base, n):
                def part(k):
                    act.wait_ge(var_ready, k + (base + 1))
                    act_fn(stat[:, 1, ds(k * n, n)], stat[:, 1, ds(k * n, n)], ACT.Sqrt, bias=eps[:, :], scale=1.0 / F).then_inc(root_ready, 1)
                return part

            skewed(act, CHUNKS, [(update_gelu, 1), (agg_copy(0, F + 1, p_u, 0), 0)])
            act.wait_ge(var_ready, 1)
            act_fn(dinv[:, :], deg[:, :], ACT.Sqrt)
            act_fn(vec[:, 6:7], vec[:, 5:6], ACT.Sqrt, bias=eps[0:F, :])
            act_fn(stat[:, 1, :], stat[:, 1, :], ACT.Sqrt, bias=eps[:, :], scale=1.0 / F).then_inc(root_ready, 1)
            skewed(act, GROUPS, [(squares(X, 0, GB), 0), (roots(1, GB), 1)])

            def ct_copy(i, h):
                act.wait_ge(ct_done, i * 2 + h + 3)
                act.wait_ge(msg_done, i * 2 + h + 1)
                act_fn(CT[:, HALF * h:HALF * h + HALF, :], PS[2 + h][:, :].rearrange("p (t e) -> p t e", e=P), ACT.Copy).then_inc(ct_ev, 1)

            def msg_copy(i, h, again):
                act.wait_ge(msg_done, i * 2 + h + 3)
                if again:
                    for u in range(HALF * h, HALF * h + HALF):
                        act.wait_ge(s_sc[u], i * 16)
                act_fn(MSG[:, HALF * h:HALF * h + HALF, :], PS[4 + h][:, 0:HALF * F].rearrange("p (t f) -> p t f", f=F), ACT.Copy).then_inc(msg_ev, 1)

            def diags(i, h, again):
                if again:
                    act.wait_ge(bc_done, i * 2 + h + 1)
                for u in range(HALF):
                    slot = HALF * h + u
                    last = act_fn(DIAG[:, slot, :], ident[:, :], ACT.Copy, scale=meta(0, i * 8 + slot, 1))
                last.then_inc(diag_ready, 1)

            act.wait_ge(x_ready, 1)
            for h in range(2):
                diags(0, h, False)
            for h in range(2):
                diags(1, h, True)
                ct_copy(0, h)
                msg_copy(0, h, False)
            with act.Fori(1, PAIRS - 1) as i:
                for h in range(2):
                    diags(i + 1, h, True)
                    ct_copy(i, h)
                    msg_copy(i, h, True)
            for h in range(2):
                ct_copy(PAIRS - 1, h)
                msg_copy(PAIRS - 1, h, True)

            def stage(p, i, h):
                act.wait_ge(idx_staged, i * 2 + (STAGES * (p - 2) + h))
                act_fn(idx_st[:, HALF * h:HALF * h + HALF], meta(0, i * 8 + HALF * h, HALF), ACT.Copy).then_inc(idx_staged, 1)

            def stagings(p):
                act.wait_ge(x_ready, p)
                for h in range(2):
                    act_fn(idx_st[:, HALF * h:HALF * h + HALF], meta(0, HALF * h, HALF), ACT.Copy).then_inc(idx_staged, 1)
                with act.Fori(0, PAIRS) as i:
                    for h in range(2):
                        act.wait_ge(s_g[p][h], i * 64 + 64)
                        stage(p, i + 1, h)

            skewed(act, GROUPS, [(squares(X, GROUPS, GB), 0), (roots(GROUPS + 1, GB), 1), (self_loops(scaled, 0, GB), 4)])
            stagings(2)
            def conv1_bias(k):
                act.wait_ge(p_gt, k + 2)
                act.wait_ge(lk_done, k + 1)
                act_fn(GT, PS[4][0:F, :], ACT.Identity, bias=vec[:, 1:2]).then_inc(z2_ev, 1)

            skewed(act, CHUNKS, [(self_loops(h_done, CHUNKS + 1, CH), 3), (conv1_bias, 1), (agg_copy(CHUNKS, F, p_gt, 0), 0)])
            stagings(3)
            skewed(act, GROUPS, [(squares(X, 2 * GROUPS, GB), 0), (roots(2 * GROUPS + 1, GB), 1)])
            stagings(4)
            skewed(act, CHUNKS, [(agg_copy(2 * CHUNKS, F, p_up, 2 * CHUNKS), 0), (squares(AGG, 3 * GROUPS, CH), 3), (roots(3 * GROUPS + 1, CH), 4)])

        @block.vector
        def _(dve):
            step = chain(dve, dve_step)
            v = nc.vector
            dve.sem_inc(z_added, 4)
            dve.sem_inc(same_ready, 2)
            dve.sem_inc(agg_added, 8)
            for s in (x_ev, h_done, lk_done, bn_ready):
                dve.sem_inc(s, 1)
            dve.sem_inc(t0_ev, T0_SLOTS)
            dve.sem_inc(hist_step, 1)
            v.memset(Zf[F:F + 1, 0:T0_SLOTS * 2 * P], 1.0).then_inc(ones_row, 1)
            dve.wait_ge(const_ready, 12)
            step(v.tensor_copy(iota_row[:, :], iota_i[:, :]))
            step(v.tensor_copy(tile_id[:, :], tile_id_i[:, :]))
            step(v.tensor_tensor(ident[:, :], iota_i[:, :], part_i[:, :], ALU.is_equal))
            step(v.tensor_tensor(earlier[:, :], iota_i[:, :], part_i[:, :], ALU.is_lt))
            step(v.tensor_copy(spare[:, :], spare_i[:, :]))

            step(v.tensor_scalar(minus_bin[:, :], iota_row[:, :], -1.0, 0.5, ALU.mult, ALU.add))
            dve.wait_ge(s_pm, 16)
            step(v.tensor_single_scalar(hi_i, pm_dst, 7, ALU.logical_shift_right))
            step(v.tensor_copy(hi_f, hi_i))
            dve.engine_nop().then_inc(hi_ready, 1)

            def count_bin(b):
                dve.wait_ge(hist_step, b + 1)
                v.tensor_scalar(hjunk, hi_f, iota_row[:, ds(b, 1)], None, ALU.is_equal, ALU.add,
                                accum_out=cnt[:, ds(b, 1)]).then_inc(hist_step, 1)

            def t0_copy(i, j, again):
                dve.wait_ge(t0_mm, i * T0_SLOTS + j + T0_SLOTS + 1)
                if again:
                    dve.wait_ge(s_t0[j], i * 16)
                v.tensor_copy(T0S[j], t0_bank[j][:, 0:4 * F]).then_inc(t0_ev, 1)

            for j in range(T0_SLOTS):
                t0_copy(0, j, False)
            with dve.Fori(1, T0_ROUNDS) as i:
                for b in range(BINS_ROUND):
                    count_bin(i * BINS_ROUND + (b - BINS_ROUND))
                for j in range(T0_SLOTS):
                    t0_copy(i, j, True)
            with dve.Fori(BINS_ROUND * (T0_ROUNDS - 1), BINS_DVE) as b:
                count_bin(b)
            dve.wait_ge(hist_step, BINS_DVE + 1)
            dve.engine_nop().then_inc(cnt_ready, 1)
            dve.wait_ge(fold_mm, 1)
            v.tensor_copy(W2T[:, :], PS[2][0:F, 0:F + 1]).then_inc(fold_ev, 1)
            c, nt, ti, dg, one = (row_f[:, k, :] for k in range(5))
            step(v.memset(one, 1.0))
            dve.wait_ge(tot_ready, 1)
            step(v.tensor_copy(c, PS[6][:, 0:BINS]))
            step(v.tensor_tensor(nt[:, BINS_DVE:NREAL], c[:, BINS_DVE:NREAL], c[:, BINS_DVE + 1:BINS], ALU.subtract))
            step(v.tensor_scalar(c[:, BINS_DVE:NREAL], nt[:, BINS_DVE:NREAL], 0.5, None, ALU.mult))
            step(v.memset(c[:, NREAL:BINS], 0.0))
            step(v.tensor_scalar(row_i[:, 0, :], c, 127.0, None, ALU.add))
            step(v.tensor_single_scalar(row_i[:, 1, :], row_i[:, 0, :], 7, ALU.logical_shift_right))
            step(v.tensor_copy(nt, row_i[:, 1, :]))
            step(v.tensor_tensor_scan(ti, one, nt, 0.0, ALU.mult, ALU.add))
            step(v.scalar_tensor_tensor(dg, nt, -128.0, c, ALU.mult, ALU.add))
            for k in range(TCH):
                v.tensor_scalar(junk[:, 0, :], ti, tile_id[:, k:k + 1], None, ALU.is_le, ALU.add,
                                accum_out=tcol[:, 0, k:k + 1])
                step(v.scalar_tensor_tensor(junk[:, 1, :], ti, tile_id[:, k:k + 1], dg, ALU.is_le, ALU.mult,
                                            accum_out=tcol[:, 1, k:k + 1]))
            step(v.tensor_scalar(tcol[:, 0, :], tcol[:, 0, :], float(NREAL), None, ALU.min))
            step(v.scalar_tensor_tensor(tcol[:, 1, :], tile_id[:, :], 128.0, tcol[:, 1, :], ALU.mult, ALU.add))
            step(v.tensor_scalar(tcol[:, 1, :], tcol[:, 1, :], float(EPAD - P), None, ALU.min))
            step(v.tensor_scalar(tcol[:, 2, :], tcol[:, 0, :], 128.0, None, ALU.mult))
            step(v.tensor_copy(tcol_i[:, :], tcol[:, 1, :]))
            dve.engine_nop().then_inc(tiles_known, 1)
            dve.wait_ge(fold_mm, 2)
            step(v.tensor_copy(WU[:, :], PS[3][0:F + 1, 0:F]))
            dve.wait_ge(tcol_t, 1)
            step(v.tensor_copy(tp_i[:, :], PS[7][0:2 * TCH, 0:P]))
            dve.engine_nop().then_inc(trow_out, 1)

            dve.wait_ge(s_rows[0], 16 * TCH)
            src_i = ROWS[:, 0, :, :].bitcast(i32)
            step(v.tensor_single_scalar(ROWI[:, 0, :, :], src_i, 127, ALU.bitwise_and))
            step(v.tensor_single_scalar(ROWI[:, 1, :, :], src_i, 7, ALU.logical_shift_right))
            step(v.scalar_tensor_tensor(ROWS[:, 0, :, :], ROWI[:, 0, :, :], float(NB), ROWI[:, 1, :, :], ALU.mult, ALU.add))
            dve.wait_ge(s_rows[1], 16 * TCH)
            step(v.tensor_copy(ROWI[:, 0, :, :], ROWS[:, 1, :, :].bitcast(i32)))
            dve.wait_ge(s_rows[2], 16 * TCH)
            v.tensor_tensor(ROWS[:, 1, :, :], ROWI[:, 0, :, :], tcol[:, 2, :].unsqueeze(2).to_broadcast([P, TCH, P]),
                            ALU.subtract).then_inc(rows_f, 1)
            for c in range(TCH):
                dve.wait_ge(rows_t, c + 1)
                v.tensor_copy(MD[:, :, c * P:(c + 1) * P], seg_bank[c % 2][:, 0:3 * P].rearrange("p (k e) -> p k e", k=3)).then_inc(md_ready, 1)
            dve.wait_ge(md_ready, TCH)
            dve.wait_ge(s_trow, 32)

            def blocks(col):
                _, b = nc.values_load_multi_w_load_instructions(
                    tile_row[0:1, ds(col, 8)], engines=[DVE], min_val=0, max_val=NREAL,
                    skip_runtime_bounds_check_because="the block of a tile is clamped to NREAL when it is computed")
                return b

            def one_hot(p, i, h, u):
                slot = HALF * h + u
                if WEIGHTED[p]:
                    ins = v.tensor_scalar(S[:, slot, :], iota_row[:, :], meta(1, i * 8 + slot, 1), meta(2, i * 8 + slot, 1), ALU.is_equal, ALU.mult)
                    if u == HALF - 1:
                        ins.then_inc(s_ready, 1)
                elif u == 0:
                    v.tensor_tensor(S[:, slot:slot + HALF, :], iota_row[:, :].unsqueeze(1).to_broadcast([P, HALF, P]),
                                    meta(1, i * 8 + slot, HALF).unsqueeze(2).to_broadcast([P, HALF, P]), ALU.is_equal).then_inc(s_ready, 1)

            def add(p, i, h, u, b, width):
                dve.wait_ge(agg_added, i * 8 + (TILES * turn(p) + HALF * h + u + 8))
                sums = AGG[:, ds(b[HALF * h + u], 1), 0:width].rearrange("p b f -> p (b f)")
                v.tensor_tensor(sums, sums, seg_bank[h][:, u * P:u * P + width], ALU.add).then_inc(agg_added, 1)

            def hots_and_adds(p, hot, add_, b, width):
                if hot:
                    dve.wait_ge(seg_done, hot[0] * 2 + (HALVES * turn(p) + hot[1] + 1))
                if add_:
                    dve.wait_ge(seg_done, add_[0] * 2 + (HALVES * turn(p) + add_[1] + 3))
                for u in range(HALF):
                    if add_:
                        add(p, add_[0], add_[1], u, b, width)
                    if hot:
                        one_hot(p, hot[0], hot[1], u)

            def z_add(i, h):
                dve.wait_ge(z_mm, i * 2 + h + 3)
                if not isinstance(i, int) or i > 0:
                    dve.wait_ge(h_ready, i * 2 + h - 1)
                for k in range(2):
                    sl = slice(HALF * h + 2 * k, HALF * h + 2 * k + 2)
                    dve.wait_ge(s_two[h][k], i * 32 + 32)
                    v.tensor_tensor(Z[:, sl, :], G[:, sl, :], z_bank[h][k][:, 0:384].rearrange("p (t f) -> p t f", t=2), ALU.add).then_inc(z_added, 1)

            def gate_lin(i, h):
                dve.wait_ge(h_ready, i * 2 + h + 1)
                sl = slice(HALF * h, HALF * h + HALF)
                if not (isinstance(i, int) and i == 0 and h == 0):
                    dve.wait_ge(lin_ready, i * 2 + h)
                for u in range(HALF):
                    slot = HALF * h + u
                    last = v.tensor_tensor_reduce(out=prod[:, u, :], in0=H[:, slot, 0:F], in1=gw2[:, :], scale=1.0, scalar=0.0,
                                                  op0=ALU.mult, op1=ALU.add, accum_out=glin[:, slot:slot + 1])
                last.then_inc(lin_ready, 1)

            def late_blocks(i):
                b = list(blocks(i * 8 - HALF))
                return b[HALF:] + b[:HALF]

            z_add(0, 0)
            z_add(0, 1)
            gate_lin(0, 0)
            hots_and_adds(0, (0, 0), None, None, MW)
            z_add(1, 0)
            gate_lin(0, 1)
            hots_and_adds(0, (0, 1), None, None, MW)
            z_add(1, 1)
            gate_lin(1, 0)
            b = list(blocks(0))
            hots_and_adds(0, (1, 0), (0, 0), b, MW)
            with dve.Fori(2, PAIRS) as i:
                b = late_blocks(i - 1)
                z_add(i, 0)
                gate_lin(i - 1, 1)
                hots_and_adds(0, (i - 1, 1), (i - 2, 1), b, MW)
                z_add(i, 1)
                gate_lin(i, 0)
                hots_and_adds(0, (i, 0), (i - 1, 0), b, MW)
            L = PAIRS - 1
            gate_lin(L, 1)
            b = late_blocks(L)
            hots_and_adds(0, (L, 1), (L - 1, 1), b, MW)
            hots_and_adds(0, None, (L, 0), b, MW)
            b = list(blocks(L * 8))
            hots_and_adds(0, None, (L, 1), b, MW)
            dve.wait_ge(agg_added, TILES + 8)
            dve.wait_ge(m_ready, HALVES)
            v.memset(Hf[F:F + 1, 0:512], 1.0).then_inc(ones_row, 1)
            step(v.tensor_scalar(deg[:, :], AGG[:, :, MW - 1:MW].rearrange("p b f -> p (b f)"), 1.0, None, ALU.add))
            dve.engine_nop().then_inc(pass_done, 1)

            def add_update(k):
                dve.wait_ge(p_up, k + 2)
                v.tensor_tensor(AGG[:, ds(k * CH, CH), 0:F], X[:, ds(k * CH, CH), :],
                                PS[6][:, 0:CH * F].rearrange("p (k f) -> p k f", k=CH), ALU.add).then_inc(h_done, 1)

            def ln_chain(first, each, k):
                count = [0]

                def ln(ins=None):
                    if ins is None:
                        assert count[0] == each
                        return
                    count[0] += 1
                    ins.then_inc(ln_step, 1)
                    dve.wait_ge(ln_step, k * each + (first + count[0]))
                return ln

            def per_row(x, blk, n):
                return x[:, blk].unsqueeze(2).to_broadcast([P, n, F])

            def centre(ln, Y, k, n):
                blk = ds(k * n, n)
                ln(v.reduce_sum(stat[:, 0, blk], Y[:, blk, 0:F], axis=AX.X))
                return v.scalar_tensor_tensor(Y[:, blk, 0:F], per_row(stat[:, 0, :], blk, n), -1.0 / F, Y[:, blk, 0:F], ALU.mult, ALU.add)

            def variances(base, n):
                def part(k):
                    dve.wait_ge(squared, k + (base + 1))
                    v.reduce_sum(stat[:, 1, ds(k * n, n)], TX[:, ds(k * n, n), :], axis=AX.X).then_inc(var_ready, 1)
                return part

            def normalise(Y, base, n):
                def part(k):
                    blk = ds(k * n, n)
                    dve.wait_ge(root_ready, k + (base + 2))
                    v.reciprocal(stat[:, 2, blk], stat[:, 1, blk]).then_inc(scale_ready, 1)
                    dve.wait_ge(scale_ready, k + (base + 1))
                    v.tensor_tensor(X[:, blk, :], Y[:, blk, 0:F], per_row(stat[:, 2, :], blk, n), ALU.mult).then_inc(normed, 1)
                return part

            def update_moments(k):
                ln = ln_chain(0, 4, k)
                blk = ds(k * CH, CH)
                dve.wait_ge(h_done, k + 2)
                v.tensor_tensor(X[:, blk, :], X[:, blk, :], lnb[:, :].unsqueeze(1).to_broadcast([P, CH, F]), ALU.add)
                ln(centre(ln, AGG, k, CH))
                ln(v.tensor_tensor(TX[:, blk, :], AGG[:, blk, 0:F], AGG[:, blk, 0:F], ALU.mult))
                v.tensor_tensor(AGG[:, blk, 0:F], AGG[:, blk, 0:F], lng[:, :].unsqueeze(1).to_broadcast([P, CH, F]), ALU.mult)
                ln(v.reduce_sum(stat[:, 1, blk], TX[:, blk, :], axis=AX.X))
                ln()

            dve.wait_ge(s_x, 16)
            skewed(dve, CHUNKS, [(add_update, 2), (update_moments, 3)])
            ln_steps = CHUNKS * 4
            dve.engine_nop().then_inc(var_ready, 1)
            dve.wait_ge(root_ready, 1)
            step(v.reciprocal(stat[:, 2, :], stat[:, 1, :]))
            step(v.reciprocal(dinv[:, :], dinv[:, :]))

            def residual(k):
                ln = ln_chain(ln_steps, 3, k)
                blk = ds(k * GB, GB)
                ln(v.tensor_tensor(AGG[:, blk, 0:F], AGG[:, blk, 0:F], per_row(stat[:, 2, :], blk, GB), ALU.mult))
                ln(v.tensor_tensor(X[:, blk, :], X[:, blk, :], AGG[:, blk, 0:F], ALU.add))
                centre(ln, X, k, GB).then_inc(centred, 1)
                ln()

            skewed(dve, GROUPS, [(residual, 0), (variances(0, GB), 1), (normalise(X, 0, GB), 2)])
            ln_steps += GROUPS * 3
            dve.wait_ge(normed, GROUPS)
            dve.engine_nop().then_inc(x_ready, 1)
            Xa = X[:, :, :]

            def hots(i, h, again):
                if again:
                    dve.wait_ge(ct_done, i * 2 + h + 1)
                for u in range(HALF):
                    slot = HALF * h + u
                    v.tensor_scalar(S[:, slot, :], iota_row[:, :], meta(1, i * 8 + slot, 1), meta(2, i * 8 + slot, 1),
                                    ALU.is_equal, ALU.mult)

            def same_and_places(i, h, again):
                J = i * 2 + h
                sl = slice(HALF * h, HALF * h + HALF)
                dve.wait_ge(bc_done, J + 3)
                dve.wait_ge(ct_done, J + 1)
                v.tensor_tensor(SAME[:, sl, :], PS[h][:, :].rearrange("p (t e) -> p t e", e=P),
                                meta(0, i * 8 + HALF * h, HALF).unsqueeze(2).to_broadcast([P, HALF, P]), ALU.is_equal).then_inc(same_ready, 1)
                dve.wait_ge(same_ready, J + 3)
                v.tensor_scalar(from_spare[:, sl], meta(0, i * 8 + HALF * h, HALF), spare[:, 0:1], None, ALU.subtract)
                for u in range(HALF):
                    slot = HALF * h + u
                    last = v.tensor_tensor_reduce(out=EARLY[:, u, :], in0=SAME[:, slot, :], in1=earlier[:, :], scale=1.0, scalar=0.0,
                                                  op0=ALU.mult, op1=ALU.add, accum_out=repeats[:, slot:slot + 1])
                last.then_inc(rep_done, 1)
                dve.wait_ge(rep_done, J + 1)
                v.scalar_tensor_tensor(first[:, sl], repeats[:, sl], 0.0, from_spare[:, sl], ALU.is_equal, ALU.mult).then_inc(first_done, 1)
                dve.wait_ge(first_done, J + 1)
                if again:
                    for u in range(HALF * h, HALF * h + HALF):
                        dve.wait_ge(s_sc[u], i * 16)
                v.tensor_scalar(idx_st[:, sl], first[:, sl], spare[:, 0:1], None, ALU.add).then_inc(sc_idx, 1)

            dve.wait_ge(idx_two, 2 * STAGES)
            hots(0, 0, False)
            hots(0, 1, False)
            same_and_places(0, 0, False)
            hots(1, 0, True)
            same_and_places(0, 1, False)
            with dve.Fori(1, PAIRS - 1) as i:
                hots(i, 1, True)
                same_and_places(i, 0, True)
                hots(i + 1, 0, True)
                same_and_places(i, 1, True)
            hots(PAIRS - 1, 1, True)
            same_and_places(PAIRS - 1, 0, True)
            same_and_places(PAIRS - 1, 1, True)
            for k in range(COPIES):
                for q in range(2):
                    part = slice(q * NB // 2, (q + 1) * NB // 2)
                    dve.wait_ge(s_back[k % 2][q], 16 * (k // 2 + 1))
                    if k >= 1:
                        dve.wait_ge(copy_added, 2 * (k - 1) + q + 1)
                    v.tensor_tensor(X[:, part, :], X[:, part, :], (AC, TX)[k % 2][:, part, :], ALU.add).then_inc(copy_added, 1)
            dve.wait_ge(copy_added, 2 * COPIES)

            def tile_pass(p):
                dve.wait_ge(agg_set, AGG_PARTS[p])
                hots_and_adds(p, (0, 0), None, None, F)
                with dve.Fori(0, PAIRS - 1) as i:
                    b = blocks(i * 8)
                    hots_and_adds(p, (i, 1), (i, 0), b, F)
                    hots_and_adds(p, (i + 1, 0), (i, 1), b, F)
                b = blocks((PAIRS - 1) * 8)
                hots_and_adds(p, (PAIRS - 1, 1), (PAIRS - 1, 0), b, F)
                hots_and_adds(p, None, (PAIRS - 1, 1), b, F)
                dve.wait_ge(agg_added, TILES * (turn(p) + 1) + 8)

            def norm(k):
                ln = ln_chain(ln_steps, 1, k)
                centre(ln, X, k, GB).then_inc(centred, 1)
                ln()

            def scaled_rows(k):
                dve.wait_ge(normed, k + (GROUPS + 1))
                v.tensor_tensor(TX[:, ds(k * GB, GB), :], X[:, ds(k * GB, GB), :],
                                dinv[:, ds(k * GB, GB)].unsqueeze(2).to_broadcast([P, GB, F]), ALU.mult).then_inc(scaled, 1)

            skewed(dve, GROUPS, [(norm, 0), (variances(GROUPS, GB), 1), (normalise(X, GROUPS, GB), 2), (scaled_rows, 3)])
            ln_steps += GROUPS
            step(v.reciprocal(vec[:, 6:7], vec[:, 6:7]))
            step(v.tensor_tensor(vec[:, 6:7], vec[:, 6:7], vec[:, 2:3], ALU.mult))
            step(v.tensor_tensor(vec[:, 7:8], vec[:, 6:7], vec[:, 4:5], ALU.mult))
            step(v.tensor_tensor(vec[:, 7:8], vec[:, 3:4], vec[:, 7:8], ALU.subtract))
            dve.wait_ge(scaled, GROUPS)
            dve.engine_nop().then_inc(x_ready, 1)
            tile_pass(2)
            dve.engine_nop().then_inc(pass_done, 1)
            def leaky_norm(k):
                dve.wait_ge(z2_ev, k + 2)
                dve.wait_ge(bn_ready, k + 1)
                v.scalar_tensor_tensor(XT[0:F, :], GT, 0.05, GT, ALU.mult, ALU.max).then_inc(lk_done, 1)
                dve.wait_ge(lk_done, k + 2)
                dve.wait_ge(p_up, k + CHUNKS + 1)
                v.tensor_scalar(YT, XT[0:F, :], vec[:, 6:7], vec[:, 7:8], ALU.mult, ALU.add).then_inc(bn_ready, 1)

            def conv2_scaled(k):
                dve.wait_ge(p_up, k + CHUNKS + 2)
                v.tensor_tensor(TX[:, ds(k * CH, CH), :], PS[6][:, 0:CH * F].rearrange("p (k f) -> p k f", k=CH),
                                dinv[:, ds(k * CH, CH)].unsqueeze(2).to_broadcast([P, CH, F]), ALU.mult).then_inc(h_done, 1)

            skewed(dve, CHUNKS, [(conv2_scaled, 2), (leaky_norm, 1)])
            dve.wait_ge(h_done, 2 * CHUNKS + 1)
            dve.engine_nop().then_inc(x_ready, 1)
            step(v.tensor_tensor(Xa, Xa, b2r[:, :].unsqueeze(1).to_broadcast([P, NB, F]), ALU.add))
            tile_pass(3)
            dve.engine_nop().then_inc(pass_done, 1)

            def add_norm(k):
                ln = ln_chain(ln_steps, 3, k)
                blk = ds(k * GB, GB)
                ln(v.tensor_tensor(AGG[:, blk, 0:F], AGG[:, blk, 0:F], per_row(dinv, blk, GB), ALU.mult))
                ln(v.tensor_tensor(X[:, blk, :], X[:, blk, :], AGG[:, blk, 0:F], ALU.add))
                centre(ln, X, k, GB).then_inc(centred, 1)
                ln()

            skewed(dve, GROUPS, [(add_norm, 0), (variances(2 * GROUPS, GB), 1), (normalise(X, 2 * GROUPS, GB), 2)])
            ln_steps += GROUPS * 3
            dve.wait_ge(normed, 3 * GROUPS)
            dve.engine_nop().then_inc(x_ready, 1)
            tile_pass(4)
            v.memset(Zf[F:F + 1, 512:1024], 1.0).then_inc(ones_row, 1)
            dve.engine_nop().then_inc(pass_done, 1)
            def output_add(k):
                dve.wait_ge(p_up, k + 2 * CHUNKS + 2)
                v.tensor_tensor(AGG[:, ds(k * CH, CH), 0:F], X[:, ds(k * CH, CH), :],
                                PS[6][:, 0:CH * F].rearrange("p (k f) -> p k f", k=CH), ALU.add).then_inc(h_done, 1)

            def x_copy(k):
                dve.wait_ge(p_xt, k + 2)
                dve.wait_ge(p_up, k + 2 * CHUNKS + 1)
                v.tensor_copy(XT[0:F, :], PS[3][0:F, :]).then_inc(x_ev, 1)

            def output_norm(k):
                ln = ln_chain(ln_steps, 1, k)
                dve.wait_ge(h_done, k + 2 * CHUNKS + 2)
                centre(ln, AGG, k, CH).then_inc(centred, 1)
                ln()

            skewed(dve, CHUNKS, [(output_add, 1), (x_copy, 0), (output_norm, 2), (variances(3 * GROUPS, CH), 4), (normalise(AGG, 3 * GROUPS, CH), 5)])


NAMES = {
    "mW1": "L0_gnn_mW1", "mb1": "L0_gnn_mb1", "mW2": "L0_gnn_mW2", "mb2": "L0_gnn_mb2",
    "gW1": "L0_gnn_gW1", "gb1": "L0_gnn_gb1", "gW2": "L0_gnn_gW2", "gb2": "L0_gnn_gb2",
    "uW1": "L0_gnn_uW1", "ub1": "L0_gnn_ub1", "uW2": "L0_gnn_uW2", "ub2": "L0_gnn_ub2",
    "ln_g": "L0_gnn_ln_g", "ln_b": "L0_gnn_ln_b", "W1": "L2_gnn_W1", "b1": "L2_gnn_b1",
    "W2": "L2_gnn_W2", "b2": "L2_gnn_b2", "bn_gamma": "L2_gnn_bn_gamma", "bn_beta": "L2_gnn_bn_beta",
    "bn_mean": "L2_gnn_bn_mean", "bn_var": "L2_gnn_bn_var", "mlp_b": "L3_gnn_mlp_b",
}


def kernel(**inputs):
    import numpy as np
    import concourse.bacc as bacc
    from concourse.bass_utils import run_bass_kernel_spmd

    def padded(v, fill):
        v = np.asarray(v)
        return np.concatenate([v, np.full((EPAD - E,), fill, v.dtype)])

    x = np.zeros((NPAD, F), np.asarray(inputs["x"]).dtype)
    x[:N] = inputs["x"]
    xT = x.T
    ea = np.asarray(inputs["edge_attr_32"])
    eaT = np.zeros((EF, EPAD), ea.dtype)
    eaT[:, :E] = ea.T
    host = {
        "x": x.reshape(NB, P, F).transpose(1, 0, 2), "xT": xT, "eaT": eaT,
        "src": padded(inputs["src"], NREAL * P), "dst": padded(inputs["dst"], NREAL * P),
        "w": padded(inputs["edge_weight"], 0), "mlp_wT": np.asarray(inputs["L3_gnn_mlp_w"]).T,
    }
    for short, name in NAMES.items():
        host[short] = np.asarray(inputs[name])
    nc = bacc.Bacc("TRN2", target_bir_lowering=False, num_devices=1)
    arrays, aps = {}, {}
    for name, v in host.items():
        v = np.ascontiguousarray(v)
        arrays[f"in_{name}"] = v
        aps[name] = nc.dram_tensor(f"in_{name}", v.shape, mybir.dt.from_np(v.dtype), kind="ExternalInput").ap()
    out = nc.dram_tensor("out", (P, NB, F), mybir.dt.float32, kind="ExternalOutput").ap()
    build(nc, aps, out)
    r = run_bass_kernel_spmd(nc, [arrays], core_ids=[0])
    return np.ascontiguousarray(r.results[0]["out"].transpose(1, 0, 2).reshape(NPAD, F)[:N])
```
